# Optimizing a Trainium2 kernel written in Bass

```python
import numpy as np
import jax
import jax.numpy as jnp

def _softmax(x, axis=-1):
    return jax.nn.softmax(x, axis=axis)

def _gelu(x):
    return jax.nn.gelu(x, approximate=True)

def _silu(x):
    return jax.nn.silu(x)

def _sigmoid(x):
    return jax.nn.sigmoid(x)

def _layernorm(x, axis=-1, eps=1e-05):
    m = jnp.mean(x, axis=axis, keepdims=True)
    v = jnp.var(x, axis=axis, keepdims=True)
    return (x - m) / jnp.sqrt(v + eps)

def _scatter_add(tgt, idx, src, axis=0):
    return tgt.at[idx].add(src)

def _segment_sum(src, seg, n):
    return jax.ops.segment_sum(src, seg, n)
kernel_name = 'mk_adaln_ffn_d1_seqx_r4_00b0e8'

def setup_inputs(seed: int=0):
    np.random.seed(seed)
    _w = jnp.asarray

    def _rec_inputs():
        import jax
        import jax.numpy as jnp
        _rk = jax.random.key(seed)
        x = -0.000125 + 0.9999 * jax.random.normal(jax.random.fold_in(_rk, 1), (32, 64, 1024), jnp.float32)
        _lenS = 64 - jax.random.randint(jax.random.fold_in(_rk, 7), (32,), 0, max(1, 64 // 4) + 1, jnp.int32)
        _lenS2 = 64 - jax.random.randint(jax.random.fold_in(_rk, 8), (32,), 0, max(1, 64 // 4) + 1, jnp.int32)
        cond_128 = 0.0061147 + 1.02565 * jax.random.normal(jax.random.fold_in(_rk, 11), (32, 128), jnp.float32)
        fside_S_0 = -0.022604 + 0.987366 * jax.random.normal(jax.random.fold_in(_rk, 12), (64,), jnp.float32)
        return (x, cond_128, fside_S_0)
    x, cond_128, fside_S_0 = _rec_inputs()

    def _L0_cond_setup():
        import jax, jax.numpy as jnp
        import numpy as np
        from jax import lax
        N, C_IN, L = (32, 64, 1024)
        C_OUT, K, GROUPS = (64, 9, 4)
        C_DIM, PAD, STRIDE = (128, 4, 1)
        key = jax.random.key(seed)
        k1, k2, k3, k4, k5 = jax.random.split(key, 5)
        x = jax.random.normal(k1, (N, C_IN, L), dtype=jnp.float32)
        c = jax.random.normal(k2, (N, C_DIM), dtype=jnp.float32)
        weight = jax.random.normal(k3, (C_OUT, C_IN // GROUPS, K), dtype=jnp.float32)
        c_weight = jax.random.normal(k4, (C_OUT, C_DIM), dtype=jnp.float32)
        bias = jax.random.normal(k5, (C_OUT,), dtype=jnp.float32)
        return {'x': x, 'c': c, 'weight': weight, 'c_weight': c_weight, 'bias': bias}
    _L0_cond_all = _L0_cond_setup()
    _L0_cond_in = {k: v for k, v in _L0_cond_all.items() if k in ('weight', 'c_weight')}
    del _L0_cond_all

    def _L0_ffn_setup():
        import jax, jax.numpy as jnp
        import numpy as np
        SCALE = 16.0 / 8.0
        key = jax.random.key(seed)
        ks = jax.random.split(key, 6)
        B, S, IN, OUT, E, R = (4, 512, 1024, 1024, 4, 8)
        x = jax.random.normal(ks[0], (B, S, IN), dtype=jnp.float32)
        W = jax.random.normal(ks[1], (OUT, IN), dtype=jnp.float32) * 0.02
        b = jax.random.normal(ks[2], (OUT,), dtype=jnp.float32) * 0.02
        A = jax.random.normal(ks[3], (E, R, IN), dtype=jnp.float32) * 0.02
        Bm = jax.random.normal(ks[4], (E, OUT, R), dtype=jnp.float32) * 0.02
        Wr = jax.random.normal(ks[5], (E, IN), dtype=jnp.float32) * 0.02
        return {'x': x, 'W': W, 'b': b, 'A': A, 'Bm': Bm, 'Wr': Wr}
    _L0_ffn_all = _L0_ffn_setup()
    _L0_ffn_in = {k: v for k, v in _L0_ffn_all.items() if k in ('W', 'b', 'A', 'Bm', 'Wr')}
    del _L0_ffn_all
    return {'x': x, 'cond_128': cond_128, 'fside_S_0': fside_S_0, 'L0_cond_weight': _L0_cond_in['weight'], 'L0_cond_c_weight': _L0_cond_in['c_weight'], 'L0_ffn_W': _L0_ffn_in['W'], 'L0_ffn_b': _L0_ffn_in['b'], 'L0_ffn_A': _L0_ffn_in['A'], 'L0_ffn_Bm': _L0_ffn_in['Bm'], 'L0_ffn_Wr': _L0_ffn_in['Wr']}

def reference(x, cond_128, fside_S_0, L0_cond_weight, L0_cond_c_weight, L0_ffn_W, L0_ffn_b, L0_ffn_A, L0_ffn_Bm, L0_ffn_Wr):
    import jax
    import jax.numpy as jnp

    def _L0_cond_ref(x, c, weight, c_weight, bias):
        import jax, jax.numpy as jnp
        import numpy as np
        from jax import lax
        N, C_IN, L = (32, 64, 1024)
        C_OUT, K, GROUPS = (64, 9, 4)
        C_DIM, PAD, STRIDE = (128, 4, 1)
        out = lax.conv_general_dilated(x, weight, window_strides=(STRIDE,), padding=[(PAD, PAD)], dimension_numbers=('NCH', 'OIH', 'NCH'), feature_group_count=GROUPS)
        ctx = jnp.einsum('nd,od->no', c, c_weight)
        out = out + ctx[:, :, None] + bias[None, :, None]
        return out

    def _L0_ffn_ref(x, W, b, A, Bm, Wr):
        import jax, jax.numpy as jnp
        import numpy as np
        SCALE = 16.0 / 8.0
        base_out = jnp.einsum('bsi,oi->bso', x, W) + b
        gates = jax.nn.softmax(jnp.einsum('bsi,ei->bse', x, Wr), axis=-1)
        proj_r = jnp.einsum('bsi,eri->bser', x, A)
        lora_out = jnp.einsum('bser,eor->bseo', proj_r, Bm)
        lora_mix = jnp.einsum('bse,bseo->bso', gates * SCALE, lora_out)
        return base_out + lora_mix
    x = x + _L0_ffn_ref(_L0_cond_ref(x, cond_128, L0_cond_weight, L0_cond_c_weight, fside_S_0), L0_ffn_W, L0_ffn_b, L0_ffn_A, L0_ffn_Bm, L0_ffn_Wr)
    return x

_drawn_inputs = setup_inputs


def setup_inputs(seed=0):
    import zlib

    import numpy as np

    out = dict(_drawn_inputs(seed))
    spreads = {}
    factors = {'L0_ffn_b': 30.598}
    for name, (base, spread) in spreads.items():
        noise = np.random.default_rng([zlib.crc32(name.encode()), seed]).standard_normal(out[name].shape)
        drawn = base * np.exp(spread * noise) if base else spread * noise
        out[name] = jnp.asarray(drawn.astype(out[name].dtype))
    for name, factor in factors.items():
        out[name] = (out[name] * factor).astype(out[name].dtype)
    return out
```

```python
from contextlib import ExitStack

import concourse.bass as bass
from concourse import mybir

F32 = mybir.dt.float32
F32R = mybir.dt.float32r
ALU = mybir.AluOpType
ACT = mybir.ActivationFunctionType
AX_X = mybir.AxisListType.X

P = 128
BANK = 512
UNROLL = 2
LORA_SCALE = 2.0


def adaln_ffn(nc, x, cond, bias, conv_w, c_weight, W, b, A, Bm, Wr, out):
    N, C, L = x.shape
    C_OUT, CI, K = conv_w.shape
    COND = cond.shape[1]
    M = W.shape[0]
    EXPERTS, RANK = A.shape[0], A.shape[1]
    G = C // CI
    O = C_OUT // G
    R = L // P
    HALF = R // 2
    PAIR = P // C
    TILES = N // PAIR
    ER = EXPERTS * RANK
    HEAD = EXPERTS + ER
    COLS = HEAD + M
    MT = M // P
    SPLIT = 354
    BOUNDS = [0, SPLIT, 2 * SPLIT, COLS]
    NB = len(BOUNDS) - 1
    GN = PAIR * G
    RB = BANK // P
    assert C == C_OUT and K == 2 * HALF + 1 and R * CI == P and R * O == P and PAIR == 2
    assert G * P == BANK and R == 2 * RB and COLS - 2 * SPLIT <= BANK and TILES % UNROLL == 0
    LAST = TILES - UNROLL

    G_HI, G_HI2, G_LO, ONES = 0, ER, 2 * ER, 3 * ER

    x_rows = x.rearrange("n c l -> (n c) l")
    out_rows = out.rearrange("n c l -> (n c) l")

    with ExitStack() as ctx:
        def sb(name, shape, dt=F32):
            return ctx.enter_context(nc.sbuf_tensor(name, shape, dt))

        def sem(name):
            return ctx.enter_context(nc.semaphore(name))

        x_sb = sb("x_sb", [P, 2, L])
        y_sb = sb("y_sb", [P, 2, M])
        xt = sb("xt", [P, GN, R, CI])
        xp = sb("xp", [P, GN, P + 1])
        h32 = sb("h32", [P, R, P])
        h_hi = sb("h_hi", [P, 2, R, P], F32R)
        h_lo = sb("h_lo", [P, 2, R, P], F32R)
        w_hi = sb("w_hi", [P, R, COLS], F32R)
        w_lo = sb("w_lo", [P, R, COLS], F32R)
        w_nat = sb("w_nat", [P, MT, L])
        head_nat = sb("head_nat", [HEAD, L])
        toep = sb("toep", [P, 2, G, R, O])
        band = sb("band", [C_OUT, R, 2 * R, CI])
        conv_nat = sb("conv_nat", [C_OUT, CI * K])
        cond_nat = sb("cond_nat", [N, COND])
        cw_nat = sb("cw_nat", [C_OUT, COND])
        cond_t = sb("cond_t", [COND, N + C_OUT])
        bias_sb = sb("bias_sb", [N, C_OUT])
        shift = sb("shift", [N, C_OUT])
        shift_diag = sb("shift_diag", [N, N, C_OUT])
        shift_all = sb("shift_all", [P, N * C_OUT])
        ident = sb("ident", [P, P])
        ones = sb("ones", [N, P])
        bm_nat = sb("bm_nat", [P, MT, EXPERTS, RANK])
        b_nat = sb("b_nat", [P, MT])
        up_nat = sb("up_nat", [P, MT, P])
        up = sb("up", [P, M], F32R)
        gate = sb("gate", [P, 8])
        gates = sb("gates", [P, EXPERTS])
        mixed = sb("mixed", [P, ER])
        mix_parts = sb("mix_parts", [P, P])
        mix_t = sb("mix_t", [P, P], F32R)
        ps = ctx.enter_context(nc.psum_tensor("ps", [P, 8, BANK], F32))
        SETUP_BANKS = [NB, NB + 1, NB + 2]
        PREP = 2 * NB

        x_loaded = [sem(f"x_loaded{i}") for i in range(2)]
        x_copied = sem("x_copied")
        y_stored = [sem(f"y_stored{i}") for i in range(2)]
        w_loaded = [sem(f"w_loaded{i}") for i in range(MT)]
        conv_loaded = sem("conv_loaded")
        cond_loaded = sem("cond_loaded")
        head_loaded = sem("head_loaded")
        up_loaded = sem("up_loaded")
        ident_ready = sem("ident_ready")
        pool_step = sem("pool_step")
        band_ready = sem("band_ready")
        edges_ready = sem("edges_ready")
        fill_step = sem("fill_step")
        up_parts = sem("up_parts")
        setup_done = sem("setup_done")
        act_took = sem("act_took")
        dve_took = sem("dve_took")
        w_hi_ready = sem("w_hi_ready")
        diag_ready = sem("diag_ready")
        turned = sem("turned")
        xt_ready = sem("xt_ready")
        blocked = sem("blocked")
        xp_ready = sem("xp_ready")
        conv_done = sem("conv_done")
        h_ready = sem("h_ready")
        h_hi_ready = sem("h_hi_ready")
        h_lo_ready = sem("h_lo_ready")
        head_done = sem("head_done")
        max_ready = sem("max_ready")
        exp_ready = sem("exp_ready")
        gate_step = sem("gate_step")
        mix_ready = sem("mix_ready")
        mix_turned = sem("mix_turned")
        mix_t_ready = sem("mix_t_ready")
        y_done = sem("y_done")
        y_ready = sem("y_ready")

        GATE_STEPS = 5

        SETUP = [("toep", 0), ("toep", 1), ("cond", 0), ("ctx", 0)]
        SETUP += [("shift", i) for i in range(N * C_OUT // BANK)]
        SETUP += [("head", 0)]
        SETUP += [("w", (mt, half)) for mt in range(MT) for half in range(2)]
        SETUP += [("up", 0), ("up", 1)]
        BY_ACT = ("toep", "cond", "shift", "up")

        def place(kind, index):
            return SETUP.index((kind, index))

        def setup_bank(k):
            return ps[:, SETUP_BANKS[k % 3], :]

        def taken(eng, k):
            mine = SETUP[k][0] in BY_ACT
            n = sum((kind in BY_ACT) == mine for kind, _ in SETUP[:k + 1])
            eng.wait_ge(act_took if mine else dve_took, n)

        def uses(t, buf, ago=0):
            return (t - buf - ago) * 8 + 16

        W_NEED = [0] + [-(-(BOUNDS[i + 1] - HEAD) // P) for i in range(NB)]

        def w_groups(i):
            return range(place("w", (W_NEED[i], 0)), place("w", (W_NEED[i + 1] - 1, 1)) + 1)

        block = ctx.enter_context(nc.Block())

        @block.sync
        def _(sp):
            def load_x(u, row):
                sp.dma_start(x_sb[:, u, :], x_rows[bass.ds(row, P), :]).then_inc(x_loaded[u], 16)

            sp.dma_start(conv_nat[:], conv_w.rearrange("o c k -> o (c k)")).then_inc(conv_loaded, 16)
            load_x(0, 0)
            for mt in range(MT):
                sp.dma_start(w_nat[:, mt, :], W[mt * P:(mt + 1) * P, :]).then_inc(w_loaded[mt], 16)
            load_x(1, P)

            def store(buf, row):
                sp.dma_start(out_rows[bass.ds(row, P), :], y_sb[:, buf, :]).then_inc(y_stored[buf], 16)

            def slot(t, u):
                sp.wait_ge(x_copied, t + 1)
                load_x(u, (t + 2) * P)
                sp.wait_ge(y_ready, t + 1)
                store(u, t * P)

            with sp.Fori(0, LAST // UNROLL) as pair:
                for u in range(UNROLL):
                    slot(pair * UNROLL + u, u)
            for u in range(UNROLL):
                sp.wait_ge(y_ready, LAST + u + 1)
                store(u, (LAST + u) * P)
            for buf in range(2):
                sp.wait_ge(y_stored[buf], 16 * TILES // 2)

        @block.gpsimd
        def _(pool):
            nc.gpsimd.memset(ident[:], 0.0).then_inc(pool_step, 1)
            pool.wait_ge(pool_step, 1)
            nc.gpsimd.affine_select(out=ident[:], in_=ident[:], compare_op=ALU.not_equal, fill=1.0,
                                    base=0, pattern=[[-1, P]], channel_multiplier=1).then_inc(ident_ready, 1)
            nc.gpsimd.memset(band[:], 0.0).then_inc(pool_step, 1)
            pool.wait_ge(pool_step, 2)
            pool.wait_ge(conv_loaded, 16)
            for r in range(R):
                last = nc.gpsimd.tensor_copy(band[:, r, r:r + K, :],
                                             conv_nat[:].rearrange("p (c k) -> p k c", k=K))
                last.then_inc(band_ready, 1)

        @block.tensor
        def _(pe):
            def turn(out_ap, in_ap):
                n = in_ap.shape[0]
                return pe.transpose(out_ap, in_ap, ident[0:n, 0:n])

            def turn_x(u, half):
                bank = ps[:, PREP + half, :]
                src = x_sb[:, u, :].rearrange("p (j r) -> p r j", r=R)
                for i in range(RB):
                    last = turn(bank[:, i * P:(i + 1) * P], src[:, half * RB + i, :])
                last.then_inc(turned, 1)

            def block_x(s):
                for g in range(G):
                    last = turn(ps[:, PREP + s, g * P:(g + 1) * P],
                                xt[:, s * G + g, :, :].rearrange("p r c -> p (r c)"))
                last.then_inc(blocked, 1)

            def convolve(s):
                for g in range(G):
                    for i in range(2):
                        last = pe.matmul(ps[:, PREP + s, g * P:(g + 1) * P], xp[:, s * G + g, i:i + P],
                                         toep[:, i, g, :, :].rearrange("p r o -> p (r o)"),
                                         start=(i == 0), stop=(i == 1))
                last.then_inc(conv_done, 1)

            def product(buf, i, rs):
                a, z = BOUNDS[i], BOUNDS[i + 1]
                acc = ps[:, NB * buf + i, 0:z - a]
                for r in rs:
                    for lhs, rhs in ((h_hi, w_hi), (h_hi, w_lo), (h_lo, w_hi)):
                        last = pe.matmul(acc, lhs[:, buf, r, :], rhs[:, r, a:z],
                                         start=(r == 0 and lhs is h_hi and rhs is w_hi),
                                         stop=(r == R - 1 and lhs is h_lo))
                if rs[-1] == R - 1 and i == 0:
                    last.then_inc(head_done, 1)

            def lora_up(buf, t):
                pe.wait_ge(mix_t_ready, t + 1)
                for i in range(NB):
                    a = max(BOUNDS[i], HEAD)
                    z = BOUNDS[i + 1]
                    pe.matmul(ps[:, NB * buf + i, a - BOUNDS[i]:z - BOUNDS[i]], mix_t[:], up[:, a - HEAD:z - HEAD],
                              start=False, stop=True, skip_group_check=True).then_inc(y_done, 1)

            def setup(k):
                kind, index = SETUP[k]
                bank = setup_bank(k)
                if k >= 3:
                    taken(pe, k - 3)
                if kind == "toep":
                    pe.wait_ge(band_ready, R)
                    for r in range(R):
                        src = band[:, r, index * R:(index + 1) * R, :].rearrange("p l c -> p (l c)")
                        last = turn(bank[:, r * C_OUT:(r + 1) * C_OUT], src)
                elif kind == "cond":
                    pe.wait_ge(cond_loaded, 48)
                    turn(bank[:, 0:N], cond_nat[:])
                    last = turn(bank[:, N:N + C_OUT], cw_nat[:])
                elif kind == "ctx":
                    taken(pe, place("cond", 0))
                    last = pe.matmul(bank[0:N, 0:C_OUT], cond_t[:, 0:N], cond_t[:, N:N + C_OUT],
                                     start=True, stop=True)
                elif kind == "shift":
                    if index == 0:
                        pe.wait_ge(diag_ready, 1)
                        pe.wait_ge(edges_ready, 3)
                    n = BANK // C_OUT
                    last = pe.matmul(bank, ones[:], shift_diag[:, index * n:(index + 1) * n, :]
                                     .rearrange("p n o -> p (n o)"), start=True, stop=True)
                elif kind == "head":
                    pe.wait_ge(head_loaded, 32)
                    src = head_nat[:].rearrange("p (j r) -> p r j", r=R)
                    for r in range(R):
                        last = turn(bank[:, r * HEAD:(r + 1) * HEAD], src[:, r, :])
                elif kind == "w":
                    mt, half = index
                    if half == 0:
                        pe.wait_ge(w_loaded[mt], 16)
                    src = w_nat[:, mt, :].rearrange("p (j r) -> p r j", r=R)
                    for i in range(RB):
                        last = turn(bank[:, i * P:(i + 1) * P], src[:, half * RB + i, :])
                elif kind == "up":
                    if index == 0:
                        pe.wait_ge(up_parts, 5)
                    for i in range(MT // 2):
                        last = turn(bank[:, i * P:(i + 1) * P], up_nat[:, index * MT // 2 + i, :])
                last.then_inc(setup_done, 1)

            pe.wait_ge(ident_ready, 1)
            pe.wait_ge(x_loaded[0], 16)
            turn_x(0, 0)
            turn_x(0, 1)
            setup(place("toep", 0))
            setup(place("toep", 1))
            setup(place("cond", 0))
            pe.wait_ge(xt_ready, 2)
            block_x(0)
            block_x(1)
            setup(place("ctx", 0))
            taken(pe, place("toep", 1))
            pe.wait_ge(edges_ready, 2)
            for s in range(2):
                pe.wait_ge(xp_ready, s + 1)
                convolve(s)
            for k in range(place("shift", 0), place("w", (0, 0))):
                setup(k)

            def tile(t, u, first=False, last=False):
                buf, nxt = u, 1 - u
                for i in range(NB):
                    for rs in ((0, 1), (2, 3), (4, 5), (6, 7)):
                        step = (i, rs[0])
                        if first and rs[0] == 0:
                            for k in w_groups(i):
                                setup(k)
                            taken(pe, w_groups(i)[-1])
                        if step == (0, 0):
                            pe.wait_ge(h_lo_ready, t + 1)
                        product(buf, i, rs)
                        if first and step == (2, 4):
                            setup(place("up", 0))
                            setup(place("up", 1))
                        if step == (2, 4):
                            pe.wait_ge(h_ready, 2 * t + 2)
                            pe.wait_ge(mix_ready, t + 1)
                            if not last:
                                pe.wait_ge(h_ready, 2 * t + 4)
                            turn(ps[:, PREP, 0:P], mix_parts[:]).then_inc(mix_turned, 1)
                        if last:
                            continue
                        if step == (0, 0):
                            pe.wait_ge(x_loaded[nxt], uses(t + 1, nxt))
                            if not first:
                                pe.wait_ge(mix_t_ready, t)
                            turn_x(nxt, 0)
                        if step == (0, 2):
                            pe.wait_ge(h_ready, 2 * t + 2)
                            turn_x(nxt, 1)
                        if step == (0, 6):
                            pe.wait_ge(xt_ready, 2 * t + 4)
                            block_x(0)
                            block_x(1)
                        if step == (1, 2):
                            pe.wait_ge(xp_ready, 2 * t + 3)
                            convolve(0)
                        if step == (1, 6):
                            pe.wait_ge(xp_ready, 2 * t + 4)
                            convolve(1)
                if first:
                    taken(pe, place("up", 1))
                lora_up(buf, t)

            tile(0, 0, first=True)
            tile(1, 1)
            with pe.Fori(1, LAST // UNROLL) as pair:
                for u in range(UNROLL):
                    tile(pair * UNROLL + u, u)
            for u in range(UNROLL):
                tile(LAST + u, u, last=(u == UNROLL - 1))

        @block.scalar
        def _(act):
            act.dma_start(cond_nat[:], cond).then_inc(cond_loaded, 16)
            act.dma_start(cw_nat[:], c_weight).then_inc(cond_loaded, 16)
            act.dma_start(bias_sb[:], bias.rearrange("(a o) -> a o", a=1).broadcast_to([N, C_OUT])).then_inc(cond_loaded, 16)
            act.dma_start(head_nat[0:EXPERTS, :], Wr).then_inc(head_loaded, 16)
            act.dma_start(head_nat[EXPERTS:HEAD, :], A.rearrange("e r l -> (e r) l")).then_inc(head_loaded, 16)
            for e in range(EXPERTS):
                act.dma_start(bm_nat[:, :, e, :], Bm[e].rearrange("(m p) r -> p m r", p=P)).then_inc(up_loaded, 16)
            act.dma_start(b_nat[:], b.rearrange("(m p) -> p m", p=P), allow_slow_non_contiguous=True).then_inc(up_loaded, 16)

            def take_blocks(s, n):
                act.wait_ge(blocked, n)
                src = ps[:, PREP + s, :].rearrange("p (g j) -> p g j", g=G)
                nc.scalar.copy(xp[0:P // 2, s * G:(s + 1) * G, 1:P + 1], src[0:P // 2])
                nc.scalar.copy(xp[P // 2:P, s * G:(s + 1) * G, 0:P], src[P // 2:P]).then_inc(xp_ready, 1)

            def copy_x(t, u):
                act.wait_ge(x_loaded[u], uses(t, u))
                if not isinstance(t, int) or t >= 2:
                    act.wait_ge(y_stored[u], uses(t, u, 2))
                nc.scalar.copy(y_sb[:, u, :], x_sb[:, u, :]).then_inc(x_copied, 1)

            def round_h(buf, t):
                act.wait_ge(h_ready, 2 * t + 2)
                nc.scalar.copy(h_hi[:, buf, :, :], h32[:]).then_inc(h_hi_ready, 1)

            def setup(k):
                kind, index = SETUP[k]
                bank = setup_bank(k)
                act.wait_ge(setup_done, k + 1)
                if kind == "toep":
                    nc.scalar.copy(toep[:, index, :, :, :].rearrange("p g r o -> p r g o"),
                                   bank.rearrange("p (r g o) -> p r g o", r=R, g=G)).then_inc(act_took, 1)
                elif kind == "cond":
                    nc.scalar.copy(cond_t[:], bank[:, 0:N + C_OUT]).then_inc(act_took, 1)
                elif kind == "shift":
                    nc.scalar.copy(shift_all[:, index * BANK:(index + 1) * BANK], bank).then_inc(act_took, 1)
                elif kind == "head":
                    nc.scalar.copy(w_hi[:, :, 0:HEAD],
                                   bank[:, 0:R * HEAD].rearrange("p (r c) -> p r c", r=R)).then_inc(w_hi_ready, 1)
                elif kind == "w":
                    mt, half = index
                    a = HEAD + mt * P
                    nc.scalar.copy(w_hi[:, half * RB:(half + 1) * RB, a:a + P],
                                   bank.rearrange("p (r c) -> p r c", r=RB)).then_inc(w_hi_ready, 1)
                elif kind == "up":
                    nc.scalar.copy(up[:, index * BANK:(index + 1) * BANK], bank).then_inc(act_took, 1)

            setup(place("toep", 0))
            setup(place("toep", 1))
            setup(place("cond", 0))
            take_blocks(0, 1)
            take_blocks(1, 2)
            copy_x(0, 0)
            for k in range(place("shift", 0), place("w", (0, 0))):
                setup(k)
            round_h(0, 0)
            for k in w_groups(0):
                setup(k)

            def tile(t, u, first=False, last=False):
                buf = u
                if not last:
                    take_blocks(0, 2 * t + 3)
                    take_blocks(1, 2 * t + 4)
                if first:
                    for k in w_groups(1):
                        setup(k)
                act.wait_ge(max_ready, t + 1)
                nc.scalar.activation(gate[:, 4:4 + EXPERTS], ps[:, NB * buf, 0:EXPERTS], ACT.Exp,
                                     bias=gate[:, 0:1], accum_out=gate[:, 1:2]).then_inc(exp_ready, 1)
                if not last:
                    round_h(1 - buf, t + 1)
                    copy_x(t + 1, 1 - buf)
                if first:
                    for k in w_groups(2):
                        setup(k)
                    setup(place("up", 0))
                    setup(place("up", 1))
                act.wait_ge(mix_turned, t + 1)
                nc.scalar.copy(mix_t[:], ps[:, PREP, 0:P]).then_inc(mix_t_ready, 1)

            tile(0, 0, first=True)
            tile(1, 1)
            with act.Fori(1, LAST // UNROLL) as pair:
                for u in range(UNROLL):
                    tile(pair * UNROLL + u, u)
            for u in range(UNROLL):
                tile(LAST + u, u, last=(u == UNROLL - 1))

        @block.vector
        def _(dve):
            def take_x(half, n):
                dve.wait_ge(turned, n)
                slot = (half * RB + HALF) % R
                nc.vector.tensor_copy(xt[:, :, slot:slot + RB, :].rearrange("p n r c -> p r n c"),
                                      ps[:, PREP + half, :].rearrange("p (r n c) -> p r n c", r=RB, n=GN)
                                      ).then_inc(xt_ready, 1)

            def take_conv(s, n, t):
                dve.wait_ge(conv_done, n)
                if isinstance(t, int):
                    add = shift_all[:, (t * PAIR + s) * C_OUT:(t * PAIR + s + 1) * C_OUT]
                else:
                    add = shift_all[:, bass.ds(t * (PAIR * C_OUT) + s * C_OUT, C_OUT)]
                add = add.rearrange("p (r g o) -> p r g o", r=1, g=G).broadcast_to([P, R, G, O])
                nc.vector.tensor_tensor(h32[:, :, s * C_OUT:(s + 1) * C_OUT].rearrange("p r (g o) -> p r g o", g=G),
                                        ps[:, PREP + s, :].rearrange("p (g r o) -> p r g o", g=G, r=R),
                                        add, ALU.add).then_inc(h_ready, 1)

            def split_h(buf, t):
                dve.wait_ge(h_hi_ready, t + 1)
                nc.vector.tensor_tensor(h_lo[:, buf, :, :], h32[:], h_hi[:, buf, :, :].bitcast(F32),
                                        ALU.subtract).then_inc(h_lo_ready, 1)

            def setup(k):
                kind, index = SETUP[k]
                bank = setup_bank(k)
                if kind == "ctx":
                    dve.wait_ge(setup_done, k + 1)
                    nc.vector.tensor_tensor(shift[:], bank[0:N, 0:C_OUT], bias_sb[:], ALU.add).then_inc(dve_took, 1)
                    dve.wait_ge(dve_took, 1)
                    dve.wait_ge(ident_ready, 1)
                    nc.vector.tensor_tensor(
                        shift_diag[:],
                        shift[:].rearrange("p (n o) -> p n o", n=1).broadcast_to([N, N, C_OUT]),
                        ident[0:N, 0:N].rearrange("p (n o) -> p n o", o=1).broadcast_to([N, N, C_OUT]),
                        ALU.mult).then_inc(diag_ready, 1)
                elif kind == "head":
                    dve.wait_ge(w_hi_ready, 1)
                    nc.vector.tensor_tensor(w_lo[:, :, 0:HEAD], bank[:, 0:R * HEAD].rearrange("p (r c) -> p r c", r=R),
                                            w_hi[:, :, 0:HEAD].bitcast(F32), ALU.subtract).then_inc(dve_took, 1)
                elif kind == "w":
                    mt, half = index
                    a = HEAD + mt * P
                    dve.wait_ge(w_hi_ready, 2 + 2 * mt + half)
                    rs = slice(half * RB, (half + 1) * RB)
                    nc.vector.tensor_tensor(w_lo[:, rs, a:a + P], bank.rearrange("p (r c) -> p r c", r=RB),
                                            w_hi[:, rs, a:a + P].bitcast(F32), ALU.subtract).then_inc(dve_took, 1)

            def up_columns():
                bm = bm_nat[:].rearrange("p m e r -> p m (e r)")
                bb = b_nat[:].rearrange("p (m a) -> p m a", a=1)
                dve.wait_ge(up_loaded, 16 * (EXPERTS + 1))
                dve.wait_ge(fill_step, 3)
                nc.vector.tensor_copy(up_nat[:, :, G_HI:G_HI + ER].bitcast(F32R), bm).then_inc(up_parts, 1)
                nc.vector.tensor_copy(up_nat[:, :, G_LO:G_LO + ER].bitcast(F32R), bm).then_inc(up_parts, 1)
                nc.vector.tensor_copy(up_nat[:, :, ONES:ONES + 1].bitcast(F32R), bb).then_inc(up_parts, 1)
                dve.wait_ge(up_parts, 3)
                nc.vector.tensor_tensor(up_nat[:, :, G_HI2:G_HI2 + ER], bm, up_nat[:, :, G_HI:G_HI + ER],
                                        ALU.subtract).then_inc(up_parts, 1)
                nc.vector.tensor_tensor(up_nat[:, :, ONES + 1:ONES + 2], bb, up_nat[:, :, ONES:ONES + 1],
                                        ALU.subtract).then_inc(up_parts, 1)

            nc.vector.memset(xp[0:P // 2, :, 0:1], 0.0).then_inc(edges_ready, 1)
            nc.vector.memset(xp[P // 2:P, :, P:P + 1], 0.0).then_inc(edges_ready, 1)
            nc.vector.memset(ones[:], 1.0).then_inc(edges_ready, 1)
            nc.vector.memset(mix_parts[:, ONES:P], 0.0).then_inc(fill_step, 1)
            nc.vector.memset(up_nat[:, :, ONES:P], 0.0).then_inc(fill_step, 1)
            dve.wait_ge(fill_step, 1)
            nc.vector.memset(mix_parts[:, ONES:ONES + 2], 1.0).then_inc(fill_step, 1)
            take_x(0, 1)
            take_x(1, 2)
            setup(place("ctx", 0))
            dve.wait_ge(act_took, 3 + N * C_OUT // BANK)
            take_conv(0, 1, 0)
            take_conv(1, 2, 0)
            setup(place("head", 0))
            split_h(0, 0)
            for k in w_groups(0):
                setup(k)

            def gating(buf, t):
                logits = ps[:, NB * buf, 0:EXPERTS]
                down = ps[:, NB * buf, EXPERTS:HEAD].rearrange("p (e r) -> p e r", e=EXPERTS)
                base = t * GATE_STEPS
                dve.wait_ge(head_done, t + 1)
                nc.vector.tensor_reduce(gate[:, 0:1], logits, AX_X, ALU.max, negate=True).then_inc(max_ready, 1)
                dve.wait_ge(exp_ready, t + 1)
                nc.vector.reciprocal(gate[:, 2:3], gate[:, 1:2]).then_inc(gate_step, 1)
                dve.wait_ge(gate_step, base + 1)
                nc.vector.tensor_scalar(gates[:], gate[:, 4:4 + EXPERTS], gate[:, 2:3], LORA_SCALE,
                                        ALU.mult, ALU.mult).then_inc(gate_step, 1)
                dve.wait_ge(gate_step, base + 2)
                nc.vector.tensor_tensor(mixed[:].rearrange("p (e r) -> p e r", e=EXPERTS), down,
                                        gates[:].rearrange("p (e r) -> p e r", r=1)
                                        .broadcast_to([P, EXPERTS, RANK]), ALU.mult).then_inc(gate_step, 1)
                dve.wait_ge(gate_step, base + 3)
                nc.vector.tensor_copy(mix_parts[:, G_HI:G_HI + ER].bitcast(F32R), mixed[:]).then_inc(gate_step, 1)
                nc.vector.tensor_copy(mix_parts[:, G_HI2:G_HI2 + ER].bitcast(F32R), mixed[:]).then_inc(gate_step, 1)
                dve.wait_ge(gate_step, base + 5)
                nc.vector.tensor_tensor(mix_parts[:, G_LO:G_LO + ER], mixed[:], mix_parts[:, G_HI:G_HI + ER],
                                        ALU.subtract).then_inc(mix_ready, 1)

            def finish(t, u):
                buf = u
                dve.wait_ge(x_copied, t + 1)
                for i in range(NB):
                    a, z = max(BOUNDS[i], HEAD), BOUNDS[i + 1]
                    dve.wait_ge(y_done, NB * t + i + 1)
                    last = nc.vector.tensor_tensor(y_sb[:, buf, a - HEAD:z - HEAD],
                                                   ps[:, NB * buf + i, a - BOUNDS[i]:z - BOUNDS[i]],
                                                   y_sb[:, buf, a - HEAD:z - HEAD], ALU.add)
                last.then_inc(y_ready, 1)

            def tile(t, u, first=False, last=False):
                buf = u
                if not last:
                    take_x(0, 2 * t + 3)
                    take_x(1, 2 * t + 4)
                if first:
                    for k in w_groups(1):
                        setup(k)
                if not last:
                    take_conv(0, 2 * t + 3, t + 1)
                gating(buf, t)
                if not last:
                    take_conv(1, 2 * t + 4, t + 1)
                    split_h(1 - buf, t + 1)
                if first:
                    for k in w_groups(2):
                        setup(k)
                    up_columns()
                finish(t, u)

            tile(0, 0, first=True)
            tile(1, 1)
            with dve.Fori(1, LAST // UNROLL) as pair:
                for u in range(UNROLL):
                    tile(pair * UNROLL + u, u)
            for u in range(UNROLL):
                tile(LAST + u, u, last=(u == UNROLL - 1))


_INS = ['x', 'cond_128', 'fside_S_0', 'L0_cond_weight', 'L0_cond_c_weight', 'L0_ffn_W', 'L0_ffn_b',
        'L0_ffn_A', 'L0_ffn_Bm', 'L0_ffn_Wr']
_OUTS = [((32, 64, 1024), 'float32')]


def kernel(**inputs):
    import numpy as _np
    import concourse.bacc as _bacc
    from concourse import mybir as _mybir
    from concourse.bass_utils import run_bass_kernel_spmd as _run

    nc = _bacc.Bacc("TRN2", target_bir_lowering=False, num_devices=1)
    arrays, args = {}, []
    for name in _INS:
        a = _np.ascontiguousarray(inputs[name])
        arrays[f"in_{name}_dram"] = a
        args.append(nc.dram_tensor(f"in_{name}_dram", a.shape, _mybir.dt.from_np(a.dtype), kind="ExternalInput").ap())
    for i, (shape, dtype) in enumerate(_OUTS):
        dt = _mybir.dt.from_np(_np.dtype(dtype))
        args.append(nc.dram_tensor(f"out_{i}_dram", shape, dt, kind="ExternalOutput").ap())
    adaln_ffn(nc, *args)
    r = _run(nc, [arrays], core_ids=[0])
    got = tuple(r.results[0][f"out_{i}_dram"] for i in range(len(_OUTS)))
    return got[0]
```

```python
from contextlib import ExitStack

import concourse.bass as bass
from concourse import mybir

F32 = mybir.dt.float32
F32R = mybir.dt.float32r
ALU = mybir.AluOpType
ACT = mybir.ActivationFunctionType
AX_X = mybir.AxisListType.X

P = 128
BANK = 512
UNROLL = 2
LORA_SCALE = 2.0


def adaln_ffn(nc, x, cond, bias, conv_w, c_weight, W, b, A, Bm, Wr, out):
    N, C, L = x.shape
    C_OUT, CI, K = conv_w.shape
    COND = cond.shape[1]
    M = W.shape[0]
    EXPERTS, RANK = A.shape[0], A.shape[1]
    G = C // CI
    O = C_OUT // G
    R = L // P
    HALF = R // 2
    PAIR = P // C
    TILES = N // PAIR
    ER = EXPERTS * RANK
    HEAD = EXPERTS + ER
    COLS = HEAD + M
    MT = M // P
    SPLIT = 354
    BOUNDS = [0, SPLIT, 2 * SPLIT, COLS]
    NB = len(BOUNDS) - 1
    GN = PAIR * G
    RB = BANK // P
    assert C == C_OUT and K == 2 * HALF + 1 and R * CI == P and R * O == P and PAIR == 2
    assert G * P == BANK and R == 2 * RB and COLS - 2 * SPLIT <= BANK and TILES % UNROLL == 0
    LAST = TILES - UNROLL

    G_HI, G_HI2, G_LO, ONES = 0, ER, 2 * ER, 3 * ER

    x_rows = x.rearrange("n c l -> (n c) l")
    out_rows = out.rearrange("n c l -> (n c) l")

    with ExitStack() as ctx:
        def sb(name, shape, dt=F32):
            return ctx.enter_context(nc.sbuf_tensor(name, shape, dt))

        def sem(name):
            return ctx.enter_context(nc.semaphore(name))

        x_sb = sb("x_sb", [P, 2, L])
        y_sb = sb("y_sb", [P, 2, M])
        xr = sb("xr", [P, R, P + 1])
        xp = sb("xp", [P, GN, P + 1])
        h32 = sb("h32", [P, R, P])
        h_hi = sb("h_hi", [P, 2, R, P], F32R)
        h_lo = sb("h_lo", [P, 2, R, P], F32R)
        w_hi = sb("w_hi", [P, R, COLS], F32R)
        w_lo = sb("w_lo", [P, R, COLS], F32R)
        w_nat = sb("w_nat", [P, MT, L])
        head_nat = sb("head_nat", [HEAD, L])
        toep = sb("toep", [P, 2, G, R, O])
        band = sb("band", [C_OUT, R, 2, CI, R])
        conv_nat = sb("conv_nat", [C_OUT, CI * K])
        cond_nat = sb("cond_nat", [N, COND])
        cw_nat = sb("cw_nat", [C_OUT, COND])
        cond_t = sb("cond_t", [COND, N + C_OUT])
        bias_sb = sb("bias_sb", [N, C_OUT])
        shift = sb("shift", [N, C_OUT])
        shift_hi = sb("shift_hi", [N, C_OUT], F32R)
        shift_lo = sb("shift_lo", [N, C_OUT], F32R)
        diag_hi = sb("diag_hi", [N, N, C_OUT], F32R)
        diag_lo = sb("diag_lo", [N, N, C_OUT], F32R)
        shift_all = sb("shift_all", [P, N * C_OUT])
        ident = sb("ident", [P, P])
        ones = sb("ones", [N, P], F32R)
        bm_nat = sb("bm_nat", [P, MT, EXPERTS, RANK])
        b_nat = sb("b_nat", [P, MT])
        up_nat = sb("up_nat", [P, MT, P])
        up = sb("up", [P, M], F32R)
        gate = sb("gate", [P, 8])
        gates = sb("gates", [P, EXPERTS])
        mixed = sb("mixed", [P, ER])
        mix_parts = sb("mix_parts", [P, P])
        mix_t = sb("mix_t", [P, P], F32R)
        ps = ctx.enter_context(nc.psum_tensor("ps", [P, 8, BANK], F32))
        SETUP_BANKS = [NB, NB + 1, NB + 2]
        PREP = 2 * NB

        x_loaded = [sem(f"x_loaded{i}") for i in range(2)]
        x_copied = sem("x_copied")
        y_stored = [sem(f"y_stored{i}") for i in range(2)]
        w_loaded = [sem(f"w_loaded{i}") for i in range(MT)]
        conv_loaded = sem("conv_loaded")
        cond_loaded = sem("cond_loaded")
        head_loaded = sem("head_loaded")
        up_loaded = sem("up_loaded")
        ident_ready = sem("ident_ready")
        pool_step = sem("pool_step")
        band_ready = sem("band_ready")
        edges_ready = sem("edges_ready")
        fill_step = sem("fill_step")
        up_parts = sem("up_parts")
        setup_done = sem("setup_done")
        act_took = sem("act_took")
        dve_took = sem("dve_took")
        w_hi_ready = sem("w_hi_ready")
        shift_step = sem("shift_step")
        diag_ready = sem("diag_ready")
        xr_ready = sem("xr_ready")
        xp_loaded = [sem(f"xp_loaded{s}") for s in range(PAIR)]
        conv_done = sem("conv_done")
        h_ready = sem("h_ready")
        h_hi_ready = sem("h_hi_ready")
        h_lo_ready = sem("h_lo_ready")
        head_done = sem("head_done")
        max_ready = sem("max_ready")
        exp_ready = sem("exp_ready")
        gate_step = sem("gate_step")
        mix_ready = sem("mix_ready")
        mix_turned = sem("mix_turned")
        mix_t_ready = sem("mix_t_ready")
        y_done = sem("y_done")
        y_ready = sem("y_ready")

        y_part_ready = sem("y_part_ready")

        GATE_STEPS = 5

        w_order = [("w", (mt, half)) for mt in range(MT) for half in range(2)]
        SETUP = w_order[:2] + [("toep", 0), ("toep", 1)] + w_order[2:4]
        SETUP += [("cond", 0), ("ctx", 0), ("shift", 0), ("head", 0)] + w_order[4:]
        SETUP += [("shift", i) for i in range(1, N * C_OUT // BANK)]
        SETUP += [("up", 0), ("up", 1)]
        BY_ACT = ("toep", "cond", "shift", "up")

        def place(kind, index):
            return SETUP.index((kind, index))

        def setup_bank(k):
            return ps[:, SETUP_BANKS[k % 3], :]

        def taken(eng, k):
            mine = SETUP[k][0] in BY_ACT
            n = sum((kind in BY_ACT) == mine for kind, _ in SETUP[:k + 1])
            eng.wait_ge(act_took if mine else dve_took, n)

        def hi_count(k):
            return sum(kind in ("head", "w") for kind, _ in SETUP[:k + 1])

        def uses(t, buf, ago=0):
            return (t - buf - ago) * 8 + 16

        W_NEED = [0] + [-(-(BOUNDS[i + 1] - HEAD) // P) for i in range(NB)]
        FIRST = [0] + [place("w", (W_NEED[i + 1] - 1, 1)) + 1 for i in range(NB)]
        EARLY, FOR_1, FOR_2 = (range(FIRST[i], FIRST[i + 1]) for i in range(NB))
        LATE = range(FIRST[NB], len(SETUP))
        DURING_H = 3

        block = ctx.enter_context(nc.Block())

        def move_x(eng):
            for i in range(GN):
                eng.dma_start(xp[:, i, :], xr[i * CI:(i + 1) * CI, :, :]).then_inc(xp_loaded[i // G], 16)

        def load_w(eng, mt):
            eng.dma_start(w_nat[:, mt, :], W[mt * P:(mt + 1) * P, :]).then_inc(w_loaded[mt], 16)

        @block.sync
        def _(sp):
            def load_x(u, row):
                sp.dma_start(x_sb[:, u, :], x_rows[bass.ds(row, P), :]).then_inc(x_loaded[u], 16)

            load_x(0, 0)
            sp.dma_start(conv_nat[:], conv_w.rearrange("o c k -> o (c k)")).then_inc(conv_loaded, 16)
            sp.wait_ge(edges_ready, 2)
            sp.wait_ge(xr_ready, 1)
            move_x(sp)
            load_x(1, P)
            for mt in range(W_NEED[1], MT):
                load_w(sp, mt)
            sp.wait_ge(xr_ready, 2)
            move_x(sp)

            def store(buf, row):
                sp.dma_start(out_rows[bass.ds(row, P), :], y_sb[:, buf, :]).then_inc(y_stored[buf], 16)

            def slot(t, u):
                sp.wait_ge(x_copied, t + 1)
                load_x(u, (t + 2) * P)
                sp.wait_ge(xr_ready, t + 3)
                move_x(sp)
                sp.wait_ge(y_ready, t + 1)
                store(u, t * P)

            with sp.Fori(0, LAST // UNROLL) as pair:
                for u in range(UNROLL):
                    slot(pair * UNROLL + u, u)
            sp.wait_ge(y_ready, TILES - 1)
            store(0, LAST * P)
            for i in range(NB):
                a, z = max(BOUNDS[i], HEAD) - HEAD, BOUNDS[i + 1] - HEAD
                sp.wait_ge(y_part_ready, i + 1)
                sp.dma_start(out_rows[(TILES - 1) * P:TILES * P, a:z], y_sb[:, 1, a:z]).then_inc(y_stored[1], 16)
            sp.wait_ge(y_stored[0], 16 * TILES // 2)
            sp.wait_ge(y_stored[1], 16 * (TILES // 2 - 1 + NB))

        @block.gpsimd
        def _(pool):
            nc.gpsimd.memset(ident[:], 0.0).then_inc(pool_step, 1)
            pool.wait_ge(pool_step, 1)
            nc.gpsimd.affine_select(out=ident[:], in_=ident[:], compare_op=ALU.not_equal, fill=1.0,
                                    base=0, pattern=[[-1, P]], channel_multiplier=1).then_inc(ident_ready, 1)

            pool.dma_start(cond_nat[:], cond).then_inc(cond_loaded, 16)
            pool.dma_start(cw_nat[:], c_weight).then_inc(cond_loaded, 16)
            pool.dma_start(bias_sb[:], bias.rearrange("(a o) -> a o", a=1).broadcast_to([N, C_OUT])).then_inc(cond_loaded, 16)
            pool.dma_start(head_nat[0:EXPERTS, :], Wr).then_inc(head_loaded, 16)
            pool.dma_start(head_nat[EXPERTS:HEAD, :], A.rearrange("e r l -> (e r) l")).then_inc(head_loaded, 16)
            for e in range(EXPERTS):
                pool.dma_start(bm_nat[:, :, e, :], Bm[e].rearrange("(m p) r -> p m r", p=P)).then_inc(up_loaded, 16)
            pool.dma_start(b_nat[:], b.rearrange("(m p) -> p m", p=P), allow_slow_non_contiguous=True).then_inc(up_loaded, 16)

        @block.tensor
        def _(pe):
            def turn(out_ap, in_ap):
                n = in_ap.shape[0]
                return pe.transpose(out_ap, in_ap, ident[0:n, 0:n])

            def convolve(s):
                for g in range(G):
                    for i in range(2):
                        last = pe.matmul(ps[:, PREP + s, g * P:(g + 1) * P], xp[:, s * G + g, i:i + P],
                                         toep[:, i, g, :, :].rearrange("p r o -> p (r o)"),
                                         start=(i == 0), stop=(i == 1))
                last.then_inc(conv_done, 1)

            def product(buf, i, rs):
                a, z = BOUNDS[i], BOUNDS[i + 1]
                acc = ps[:, NB * buf + i, 0:z - a]
                for r in rs:
                    for lhs, rhs in ((h_hi, w_hi), (h_hi, w_lo), (h_lo, w_hi)):
                        last = pe.matmul(acc, lhs[:, buf, r, :], rhs[:, r, a:z],
                                         start=(r == 0 and lhs is h_hi and rhs is w_hi),
                                         stop=(r == R - 1 and lhs is h_lo))
                if rs[-1] == R - 1 and i == 0:
                    last.then_inc(head_done, 1)

            def lora_up(buf, t):
                pe.wait_ge(mix_t_ready, t + 1)
                for i in range(NB):
                    a = max(BOUNDS[i], HEAD)
                    z = BOUNDS[i + 1]
                    pe.matmul(ps[:, NB * buf + i, a - BOUNDS[i]:z - BOUNDS[i]], mix_t[:], up[:, a - HEAD:z - HEAD],
                              start=False, stop=True, skip_group_check=True).then_inc(y_done, 1)

            def setup(k):
                kind, index = SETUP[k]
                bank = setup_bank(k)
                if k >= 3:
                    taken(pe, k - 3)
                if kind == "toep":
                    pe.wait_ge(band_ready, 2 * R)
                    for r in range(R):
                        last = turn(bank[:, r * C_OUT:(r + 1) * C_OUT],
                                    band[:, r, index, :, :].rearrange("p c l -> p (c l)"))
                elif kind == "cond":
                    pe.wait_ge(cond_loaded, 48)
                    turn(bank[:, 0:N], cond_nat[:])
                    last = turn(bank[:, N:N + C_OUT], cw_nat[:])
                elif kind == "ctx":
                    taken(pe, place("cond", 0))
                    last = pe.matmul(bank[0:N, 0:C_OUT], cond_t[:, 0:N], cond_t[:, N:N + C_OUT],
                                     start=True, stop=True)
                elif kind == "shift":
                    if index == 0:
                        pe.wait_ge(edges_ready, 3)
                    pe.wait_ge(diag_ready, 2 if index == 0 else 4)
                    n = BANK // C_OUT
                    for diag in (diag_hi, diag_lo):
                        last = pe.matmul(bank, ones[:], diag[:, index * n:(index + 1) * n, :]
                                         .rearrange("p n o -> p (n o)"), start=(diag is diag_hi), stop=(diag is diag_lo))
                elif kind == "head":
                    pe.wait_ge(head_loaded, 32)
                    src = head_nat[:].rearrange("p (j r) -> p r j", r=R)
                    for r in range(R):
                        last = turn(bank[:, r * HEAD:(r + 1) * HEAD], src[:, r, :])
                elif kind == "w":
                    mt, half = index
                    if half == 0:
                        pe.wait_ge(w_loaded[mt], 16)
                    src = w_nat[:, mt, :].rearrange("p (j r) -> p r j", r=R)
                    for i in range(RB):
                        last = turn(bank[:, i * P:(i + 1) * P], src[:, half * RB + i, :])
                elif kind == "up":
                    if index == 0:
                        pe.wait_ge(up_parts, 5)
                    for i in range(MT // 2):
                        last = turn(bank[:, i * P:(i + 1) * P], up_nat[:, index * MT // 2 + i, :])
                last.then_inc(setup_done, 1)

            pe.wait_ge(ident_ready, 1)
            for k in EARLY:
                setup(k)
            for s in range(PAIR):
                pe.wait_ge(xp_loaded[s], 16 * G)
                convolve(s)
            for k in FOR_1[:DURING_H]:
                setup(k)

            def tile(t, u, first=False, last=False):
                buf = u
                for i in range(NB):
                    ahead = list((FOR_1[DURING_H:], FOR_2, LATE)[i]) if first else []
                    if first:
                        taken(pe, (EARLY, FOR_1, FOR_2)[i][-1])
                    if i == 0:
                        pe.wait_ge(h_lo_ready, t + 1)
                    for r in range(R):
                        product(buf, i, (r,))
                        if ahead:
                            setup(ahead.pop(0))
                        if (i, r) == (1, 4) and not last:
                            pe.wait_ge(xp_loaded[0], 16 * G * (t + 2))
                            if not first:
                                pe.wait_ge(mix_t_ready, t)
                            convolve(0)
                        if (i, r) == (1, 6) and not last:
                            pe.wait_ge(xp_loaded[1], 16 * G * (t + 2))
                            convolve(1)
                        if (i, r) == (2, 2):
                            if not last:
                                pe.wait_ge(h_ready, 2 * t + 3)
                            pe.wait_ge(mix_ready, t + 1)
                            turn(ps[:, PREP, 0:P], mix_parts[:]).then_inc(mix_turned, 1)
                if first:
                    taken(pe, place("up", 1))
                lora_up(buf, t)

            tile(0, 0, first=True)
            tile(1, 1)
            with pe.Fori(1, LAST // UNROLL) as pair:
                for u in range(UNROLL):
                    tile(pair * UNROLL + u, u)
            for u in range(UNROLL):
                tile(LAST + u, u, last=(u == UNROLL - 1))

        @block.scalar
        def _(act):
            for mt in range(W_NEED[1]):
                load_w(act, mt)

            def reorder_x(t, u):
                act.wait_ge(x_loaded[u], uses(t, u))
                if not isinstance(t, int) or t > 0:
                    for s in range(PAIR):
                        act.wait_ge(xp_loaded[s], 16 * G * t)
                src = x_sb[:, u, :].rearrange("p (b r) -> p r b", r=R)
                nc.scalar.copy(xr[:, 0:HALF, 1:P + 1], src[:, HALF:R, :])
                nc.scalar.copy(xr[:, HALF:R, 0:P], src[:, 0:HALF, :]).then_inc(xr_ready, 1)

            def copy_x(t, u):
                if not isinstance(t, int) or t >= 2:
                    act.wait_ge(y_stored[u], uses(t, u, 2))
                nc.scalar.copy(y_sb[:, u, :], x_sb[:, u, :]).then_inc(x_copied, 1)

            def round_h(buf, t):
                act.wait_ge(h_ready, 2 * t + 2)
                nc.scalar.copy(h_hi[:, buf, :, :], h32[:]).then_inc(h_hi_ready, 1)

            def setup(k):
                kind, index = SETUP[k]
                bank = setup_bank(k)
                act.wait_ge(setup_done, k + 1)
                if kind == "toep":
                    nc.scalar.copy(toep[:, index, :, :, :].rearrange("p g r o -> p r g o"),
                                   bank.rearrange("p (r g o) -> p r g o", r=R, g=G)).then_inc(act_took, 1)
                elif kind == "cond":
                    nc.scalar.copy(cond_t[:], bank[:, 0:N + C_OUT]).then_inc(act_took, 1)
                elif kind == "shift":
                    nc.scalar.copy(shift_all[:, index * BANK:(index + 1) * BANK], bank).then_inc(act_took, 1)
                elif kind == "head":
                    nc.scalar.copy(w_hi[:, :, 0:HEAD],
                                   bank[:, 0:R * HEAD].rearrange("p (r c) -> p r c", r=R)).then_inc(w_hi_ready, 1)
                elif kind == "w":
                    mt, half = index
                    a = HEAD + mt * P
                    nc.scalar.copy(w_hi[:, half * RB:(half + 1) * RB, a:a + P],
                                   bank.rearrange("p (r c) -> p r c", r=RB)).then_inc(w_hi_ready, 1)
                elif kind == "up":
                    nc.scalar.copy(up[:, index * BANK:(index + 1) * BANK], bank).then_inc(act_took, 1)

            reorder_x(0, 0)
            for k in EARLY:
                if SETUP[k][0] != "ctx":
                    setup(k)
            round_h(0, 0)
            for k in FOR_1[:DURING_H]:
                setup(k)
            reorder_x(1, 1)
            copy_x(0, 0)

            def tile(t, u, first=False, last=False, ahead=True):
                buf = u
                if first:
                    for k in FOR_1[DURING_H:]:
                        setup(k)
                act.wait_ge(max_ready, t + 1)
                nc.scalar.activation(gate[:, 4:4 + EXPERTS], ps[:, NB * buf, 0:EXPERTS], ACT.Exp,
                                     bias=gate[:, 0:1], accum_out=gate[:, 1:2]).then_inc(exp_ready, 1)
                if first:
                    for k in FOR_2:
                        setup(k)
                if not last:
                    round_h(1 - buf, t + 1)
                if first:
                    for k in LATE[:2]:
                        setup(k)
                act.wait_ge(mix_turned, t + 1)
                nc.scalar.copy(mix_t[:], ps[:, PREP, 0:P]).then_inc(mix_t_ready, 1)
                if ahead:
                    reorder_x(t + 2, buf)
                if first:
                    for k in LATE[2:]:
                        setup(k)
                if not last:
                    copy_x(t + 1, 1 - buf)

            tile(0, 0, first=True)
            tile(1, 1)
            with act.Fori(1, LAST // UNROLL) as pair:
                for u in range(UNROLL):
                    tile(pair * UNROLL + u, u)
            for u in range(UNROLL):
                tile(LAST + u, u, last=(u == UNROLL - 1), ahead=False)

        @block.vector
        def _(dve):
            def take_conv(s, n, t):
                dve.wait_ge(conv_done, n)
                if isinstance(t, int):
                    add = shift_all[:, (t * PAIR + s) * C_OUT:(t * PAIR + s + 1) * C_OUT]
                else:
                    add = shift_all[:, bass.ds(t * (PAIR * C_OUT) + s * C_OUT, C_OUT)]
                add = add.rearrange("p (r g o) -> p r g o", r=1, g=G).broadcast_to([P, R, G, O])
                nc.vector.tensor_tensor(h32[:, :, s * C_OUT:(s + 1) * C_OUT].rearrange("p r (g o) -> p r g o", g=G),
                                        ps[:, PREP + s, :].rearrange("p (g r o) -> p r g o", g=G, r=R),
                                        add, ALU.add).then_inc(h_ready, 1)

            def split_h(buf, t):
                dve.wait_ge(h_hi_ready, t + 1)
                nc.vector.tensor_tensor(h_lo[:, buf, :, :], h32[:], h_hi[:, buf, :, :].bitcast(F32),
                                        ALU.subtract).then_inc(h_lo_ready, 1)

            def setup(k):
                kind, index = SETUP[k]
                bank = setup_bank(k)
                if kind == "ctx":
                    dve.wait_ge(setup_done, k + 1)
                    nc.vector.tensor_tensor(shift[:], bank[0:N, 0:C_OUT], bias_sb[:], ALU.add).then_inc(dve_took, 1)
                    taken(dve, k)
                    nc.vector.tensor_copy(shift_hi[:], shift[:]).then_inc(shift_step, 1)
                    dve.wait_ge(shift_step, 1)
                    nc.vector.tensor_tensor(shift_lo[:], shift[:], shift_hi[:].bitcast(F32),
                                            ALU.subtract).then_inc(shift_step, 1)
                    dve.wait_ge(ident_ready, 1)
                    dve.wait_ge(shift_step, 2)
                    diagonal(0, BANK // C_OUT)
                    diagonal(BANK // C_OUT, N)
                elif kind == "head":
                    dve.wait_ge(w_hi_ready, hi_count(k))
                    nc.vector.tensor_tensor(w_lo[:, :, 0:HEAD], bank[:, 0:R * HEAD].rearrange("p (r c) -> p r c", r=R),
                                            w_hi[:, :, 0:HEAD].bitcast(F32), ALU.subtract).then_inc(dve_took, 1)
                elif kind == "w":
                    mt, half = index
                    a = HEAD + mt * P
                    dve.wait_ge(w_hi_ready, hi_count(k))
                    rs = slice(half * RB, (half + 1) * RB)
                    nc.vector.tensor_tensor(w_lo[:, rs, a:a + P], bank.rearrange("p (r c) -> p r c", r=RB),
                                            w_hi[:, rs, a:a + P].bitcast(F32), ALU.subtract).then_inc(dve_took, 1)

            def diagonal(a, z):
                for part, diag in ((shift_hi, diag_hi), (shift_lo, diag_lo)):
                    nc.vector.tensor_tensor(
                        diag[:, a:z, :],
                        part[:].bitcast(F32).rearrange("p (n o) -> p n o", n=1).broadcast_to([N, z - a, C_OUT]),
                        ident[0:N, a:z].rearrange("p (n o) -> p n o", o=1).broadcast_to([N, z - a, C_OUT]),
                        ALU.mult).then_inc(diag_ready, 1)

            def up_columns():
                bm = bm_nat[:].rearrange("p m e r -> p m (e r)")
                bb = b_nat[:].rearrange("p (m a) -> p m a", a=1)
                dve.wait_ge(up_loaded, 16 * (EXPERTS + 1))
                dve.wait_ge(fill_step, 4)
                nc.vector.tensor_copy(up_nat[:, :, G_HI:G_HI + ER].bitcast(F32R), bm).then_inc(up_parts, 1)
                nc.vector.tensor_copy(up_nat[:, :, G_LO:G_LO + ER].bitcast(F32R), bm).then_inc(up_parts, 1)
                nc.vector.tensor_copy(up_nat[:, :, ONES:ONES + 1].bitcast(F32R), bb).then_inc(up_parts, 1)
                dve.wait_ge(up_parts, 3)
                nc.vector.tensor_tensor(up_nat[:, :, G_HI2:G_HI2 + ER], bm, up_nat[:, :, G_HI:G_HI + ER],
                                        ALU.subtract).then_inc(up_parts, 1)
                nc.vector.tensor_tensor(up_nat[:, :, ONES + 1:ONES + 2], bb, up_nat[:, :, ONES:ONES + 1],
                                        ALU.subtract).then_inc(up_parts, 1)

            nc.vector.memset(xr[:, 0:HALF, 0:1], 0.0).then_inc(edges_ready, 1)
            nc.vector.memset(xr[:, HALF:R, P:P + 1], 0.0).then_inc(edges_ready, 1)
            nc.vector.memset(ones[:].bitcast(F32), 1.0).then_inc(edges_ready, 1)
            nc.vector.memset(mix_parts[:, ONES:P], 0.0).then_inc(fill_step, 1)
            nc.vector.memset(band[:], 0.0).then_inc(fill_step, 1)
            dve.wait_ge(fill_step, 2)
            nc.vector.memset(mix_parts[:, ONES:ONES + 2], 1.0).then_inc(fill_step, 1)
            taps = conv_nat[:].rearrange("p (c k) -> p c k", k=K)
            dve.wait_ge(conv_loaded, 16)
            for r in range(R):
                nc.vector.tensor_copy(band[:, r, 0, :, r:R], taps[:, :, 0:R - r]).then_inc(band_ready, 1)
                nc.vector.tensor_copy(band[:, r, 1, :, 0:r + 1], taps[:, :, R - r:K]).then_inc(band_ready, 1)
            nc.vector.memset(up_nat[:, :, ONES:P], 0.0).then_inc(fill_step, 1)
            for k in EARLY:
                if SETUP[k][0] not in BY_ACT:
                    setup(k)
            taken(dve, place("shift", 0))
            take_conv(0, 1, 0)
            take_conv(1, 2, 0)
            split_h(0, 0)
            for k in FOR_1[:DURING_H]:
                setup(k)

            def gating(buf, t):
                logits = ps[:, NB * buf, 0:EXPERTS]
                down = ps[:, NB * buf, EXPERTS:HEAD].rearrange("p (e r) -> p e r", e=EXPERTS)
                base = t * GATE_STEPS
                dve.wait_ge(head_done, t + 1)
                nc.vector.tensor_reduce(gate[:, 0:1], logits, AX_X, ALU.max, negate=True).then_inc(max_ready, 1)
                dve.wait_ge(exp_ready, t + 1)
                nc.vector.reciprocal(gate[:, 2:3], gate[:, 1:2]).then_inc(gate_step, 1)
                dve.wait_ge(gate_step, base + 1)
                nc.vector.tensor_scalar(gates[:], gate[:, 4:4 + EXPERTS], gate[:, 2:3], LORA_SCALE,
                                        ALU.mult, ALU.mult).then_inc(gate_step, 1)
                dve.wait_ge(gate_step, base + 2)
                nc.vector.tensor_tensor(mixed[:].rearrange("p (e r) -> p e r", e=EXPERTS), down,
                                        gates[:].rearrange("p (e r) -> p e r", r=1)
                                        .broadcast_to([P, EXPERTS, RANK]), ALU.mult).then_inc(gate_step, 1)
                dve.wait_ge(gate_step, base + 3)
                nc.vector.tensor_copy(mix_parts[:, G_HI:G_HI + ER].bitcast(F32R), mixed[:]).then_inc(gate_step, 1)
                nc.vector.tensor_copy(mix_parts[:, G_HI2:G_HI2 + ER].bitcast(F32R), mixed[:]).then_inc(gate_step, 1)
                dve.wait_ge(gate_step, base + 5)
                nc.vector.tensor_tensor(mix_parts[:, G_LO:G_LO + ER], mixed[:], mix_parts[:, G_HI:G_HI + ER],
                                        ALU.subtract).then_inc(mix_ready, 1)

            def finish(t, u, parts):
                buf = u
                dve.wait_ge(x_copied, t + 1)
                for i in range(NB):
                    a, z = max(BOUNDS[i], HEAD), BOUNDS[i + 1]
                    dve.wait_ge(y_done, NB * t + i + 1)
                    last = nc.vector.tensor_tensor(y_sb[:, buf, a - HEAD:z - HEAD],
                                                   ps[:, NB * buf + i, a - BOUNDS[i]:z - BOUNDS[i]],
                                                   y_sb[:, buf, a - HEAD:z - HEAD], ALU.add)
                    if parts:
                        last.then_inc(y_part_ready, 1)
                if not parts:
                    last.then_inc(y_ready, 1)

            def tile(t, u, first=False, last=False):
                buf = u
                if first:
                    for k in FOR_1[DURING_H:]:
                        setup(k)
                gating(buf, t)
                if first:
                    up_columns()
                    for k in FOR_2:
                        setup(k)
                if not last:
                    take_conv(0, 2 * t + 3, t + 1)
                    take_conv(1, 2 * t + 4, t + 1)
                    split_h(1 - buf, t + 1)
                finish(t, u, last)

            tile(0, 0, first=True)
            tile(1, 1)
            with dve.Fori(1, LAST // UNROLL) as pair:
                for u in range(UNROLL):
                    tile(pair * UNROLL + u, u)
            for u in range(UNROLL):
                tile(LAST + u, u, last=(u == UNROLL - 1))


_INS = ['x', 'cond_128', 'fside_S_0', 'L0_cond_weight', 'L0_cond_c_weight', 'L0_ffn_W', 'L0_ffn_b',
        'L0_ffn_A', 'L0_ffn_Bm', 'L0_ffn_Wr']
_OUTS = [((32, 64, 1024), 'float32')]


def kernel(**inputs):
    import numpy as _np
    import concourse.bacc as _bacc
    from concourse import mybir as _mybir
    from concourse.bass_utils import run_bass_kernel_spmd as _run

    nc = _bacc.Bacc("TRN2", target_bir_lowering=False, num_devices=1)
    arrays, args = {}, []
    for name in _INS:
        a = _np.ascontiguousarray(inputs[name])
        arrays[f"in_{name}_dram"] = a
        args.append(nc.dram_tensor(f"in_{name}_dram", a.shape, _mybir.dt.from_np(a.dtype), kind="ExternalInput").ap())
    for i, (shape, dtype) in enumerate(_OUTS):
        dt = _mybir.dt.from_np(_np.dtype(dtype))
        args.append(nc.dram_tensor(f"out_{i}_dram", shape, dt, kind="ExternalOutput").ap())
    adaln_ffn(nc, *args)
    r = _run(nc, [arrays], core_ids=[0])
    got = tuple(r.results[0][f"out_{i}_dram"] for i in range(len(_OUTS)))
    return got[0]
```

```python
from contextlib import ExitStack

import concourse.bass as bass
from concourse import mybir

F32 = mybir.dt.float32
F32R = mybir.dt.float32r
ALU = mybir.AluOpType
ACT = mybir.ActivationFunctionType
AX_X = mybir.AxisListType.X

P = 128
BANK = 512
Q = 32
UNROLL = 4
LORA_SCALE = 2.0


def adaln_ffn(nc, x, cond, bias, conv_w, c_weight, W, b, A, Bm, Wr, out):
    N, C, L = x.shape
    C_OUT, CI, K = conv_w.shape
    COND = cond.shape[1]
    M = W.shape[0]
    EXPERTS, RANK = A.shape[0], A.shape[1]
    G = C // CI
    O = C_OUT // G
    R = L // P
    HALF = R // 2
    PAIR = P // C
    TILES = N // PAIR
    ER = EXPERTS * RANK
    HEAD = EXPERTS + ER
    COLS = HEAD + M
    MT = M // P
    SPLIT = 354
    BOUNDS = [0, SPLIT, 2 * SPLIT, COLS]
    NB = len(BOUNDS) - 1
    W_NEED = [max(0, -(-(z - HEAD) // P)) for z in BOUNDS]
    GN = PAIR * G
    RB = BANK // P
    assert C == C_OUT and K == 2 * HALF + 1 and R * CI == P and R * O == P and PAIR == 2
    assert G * P == BANK and R == 2 * RB and COLS - 2 * SPLIT <= BANK
    AHEAD = 3
    TAIL = TILES - AHEAD
    JB = P // Q
    GB = G // 2
    R2 = Q // O

    W_BUFS = MT // 2
    DIAG = BANK // C_OUT
    assert (TAIL - 1) % UNROLL == 0 and R2 * JB == R

    G_HI, G_HI2, G_LO, ONES = 0, ER, 2 * ER, 3 * ER

    x_rows = x.rearrange("n c l -> (n c) l")
    out_rows = out.rearrange("n c l -> (n c) l")

    with ExitStack() as ctx:
        def sb(name, shape, dt=F32):
            return ctx.enter_context(nc.sbuf_tensor(name, shape, dt))

        def sem(name):
            return ctx.enter_context(nc.semaphore(name))

        x_sb = sb("x_sb", [P, UNROLL, L])
        y_sb = sb("y_sb", [P, 2, M])
        xr = sb("xr", [P, R, P + 1])
        xp = sb("xp", [P, PAIR, G, P + 1])
        xp_hi = sb("xp_hi", [P, PAIR, G, P + 1], F32R)
        xp_lo = sb("xp_lo", [P, PAIR, G, P + 1], F32R)
        ht = sb("ht", [P, JB, 2, PAIR * GB, Q])
        hq = sb("hq", [P, JB, 2 * PAIR * GB * Q])
        h32 = sb("h32", [P, R, P])
        h_hi = sb("h_hi", [P, 2, R, P], F32R)
        h_lo = sb("h_lo", [P, 2, R, P], F32R)
        w_hi = sb("w_hi", [P, R, COLS], F32R)
        w_lo = sb("w_lo", [P, R, COLS], F32R)
        w_nat = sb("w_nat", [P, W_BUFS, L])
        head_nat = sb("head_nat", [HEAD, L])
        toep_hi = sb("toep_hi", [P, 2, G, R, O], F32R)
        toep_lo = sb("toep_lo", [P, 2, G, R, O], F32R)
        band = sb("band", [C_OUT, R, 2, CI, R])
        conv_nat = sb("conv_nat", [C_OUT, CI * K])
        cond_nat = sb("cond_nat", [N, COND])
        cw_nat = sb("cw_nat", [C_OUT, COND])
        cond_t = sb("cond_t", [COND, N + C_OUT])
        bias_sb = sb("bias_sb", [N, C_OUT])
        shift = sb("shift", [N, C_OUT])
        shift_hi = sb("shift_hi", [N, C_OUT], F32R)
        shift_lo = sb("shift_lo", [N, C_OUT], F32R)
        diag_hi = sb("diag_hi", [N, DIAG, C_OUT], F32R)
        diag_lo = sb("diag_lo", [N, DIAG, C_OUT], F32R)
        shift_all = sb("shift_all", [P, N * C_OUT])
        ident = sb("ident", [P, P])
        ones = sb("ones", [N, P], F32R)
        bm_nat = sb("bm_nat", [P, MT, EXPERTS, RANK])
        b_nat = sb("b_nat", [P, MT])
        up_nat = sb("up_nat", [P, MT, P])
        up = sb("up", [P, M], F32R)
        gate = sb("gate", [P, 8])
        gates = sb("gates", [P, EXPERTS])
        mixed = sb("mixed", [P, ER])
        mix_parts = sb("mix_parts", [P, P])
        mix_t = sb("mix_t", [P, P], F32R)
        ps = ctx.enter_context(nc.psum_tensor("ps", [P, 8, BANK], F32))
        PREP = 2 * NB

        x_loaded = [sem(f"x_loaded{i}") for i in range(UNROLL)]
        y_free = [sem(f"y_free{i}") for i in range(2)]
        w_loaded = [sem(f"w_loaded{i}") for i in range(MT)]
        conv_loaded = sem("conv_loaded")
        cond_loaded = sem("cond_loaded")
        head_loaded = sem("head_loaded")
        up_loaded = sem("up_loaded")
        ident_ready = sem("ident_ready")
        pool_step = sem("pool_step")
        band_ready = sem("band_ready")
        edges_ready = sem("edges_ready")
        fill_step = sem("fill_step")
        up_parts = sem("up_parts")
        setup_done = sem("setup_done")
        act_took = sem("act_took")
        dve_took = sem("dve_took")
        w_hi_ready = sem("w_hi_ready")
        shift_step = sem("shift_step")
        diag_ready = sem("diag_ready")
        xr_ready = sem("xr_ready")
        xp_loaded = sem("xp_loaded")
        xp_rest_loaded = sem("xp_rest_loaded")
        xp_hi_ready = sem("xp_hi_ready")
        xp_lo_ready = sem("xp_lo_ready")
        conv_done = sem("conv_done")
        turned = sem("turned")
        hq_loaded = sem("hq_loaded")
        h_ready = sem("h_ready")
        h_hi_ready = sem("h_hi_ready")
        h_lo_ready = sem("h_lo_ready")
        head_done = sem("head_done")
        max_ready = sem("max_ready")
        exp_ready = sem("exp_ready")
        gate_step = sem("gate_step")
        mix_ready = sem("mix_ready")
        mix_turned = sem("mix_turned")
        mix_t_ready = sem("mix_t_ready")
        y_done = sem("y_done")
        y_ready = sem("y_ready")

        y_part_ready = sem("y_part_ready")

        GATE_STEPS = 5

        w = [[("w", (mt, half)) for half in range(2)] for mt in range(MT)]
        BEFORE_0 = w[0] + [("toep", 0), ("toep", 1)] + w[1] + [("cond", 0), ("ctx", 0), ("head", 0)] + w[2]
        BEFORE_1 = w[3] + w[4] + [("shift", 0)] + w[5]
        IN_P = w[6] + w[7] + [("shift", 1), ("up", 0), ("up", 1), ("shift", 2), ("shift", 3)]
        SETUP = BEFORE_0 + BEFORE_1 + IN_P
        BY_ACT = ("cond", "shift", "up")
        SPLIT_KINDS = ("w", "head", "toep")
        n_wide = len(BEFORE_0 + BEFORE_1)
        BANKS = [k % 6 if k < n_wide else NB + k % NB for k in range(len(SETUP))]

        def place(kind, index):
            return SETUP.index((kind, index))

        def setup_bank(k):
            return ps[:, BANKS[k], :]

        def taken(eng, k):
            mine = SETUP[k][0] in BY_ACT
            n = sum((kind in BY_ACT) == mine for kind, _ in SETUP[:k + 1])
            eng.wait_ge(act_took if mine else dve_took, n)

        def hi_count(k):
            return sum(kind in SPLIT_KINDS for kind, _ in SETUP[:k + 1])

        def loads(t, m):
            return (t - m) * (16 // UNROLL) + 16

        def frees(t, b):
            return (t - b) * 8 + 16

        block = ctx.enter_context(nc.Block())

        BY_SP = (5, 3)

        def move_x(eng, pairs=range(GN), sp_moves=True):
            for sg in pairs:
                eng.dma_start(xp[:, sg // G, sg % G, :], xr[sg * CI:(sg + 1) * CI, :, :]
                              ).then_inc(xp_loaded if sp_moves else xp_rest_loaded, 16)

        def x_moved(eng, t):
            if isinstance(t, int) and t < 2:
                eng.wait_ge(xp_loaded, 16 * sum(BY_SP[:t + 1]))
                eng.wait_ge(xp_rest_loaded, 16 * (GN * (t + 1) - sum(BY_SP[:t + 1])))
            else:
                eng.wait_ge(xp_loaded, 16 * (GN * (t - 1) + sum(BY_SP)))

        def move_h(eng):
            for q in range(JB):
                eng.dma_start(hq[:, q, :], ht[q * Q:(q + 1) * Q, :, :, :, :].rearrange("p j b c i -> p j (b c i)")
                              ).then_inc(hq_loaded, 16)

        def load_w(eng, mt):
            eng.dma_start(w_nat[:, mt % W_BUFS, :], W[mt * P:(mt + 1) * P, :]).then_inc(w_loaded[mt], 16)

        @block.sync
        def _(sp):
            def load_x(m, row):
                sp.dma_start(x_sb[:, m, :], x_rows[bass.ds(row, P), :]).then_inc(x_loaded[m], 16)

            def store(b, row):
                sp.dma_start(out_rows[bass.ds(row, P), :], y_sb[:, b, :]).then_inc(y_free[b], 16)

            load_x(0, 0)
            sp.dma_start(conv_nat[:], conv_w.rearrange("o c k -> o (c k)")).then_inc(conv_loaded, 16)
            sp.wait_ge(edges_ready, 3)
            sp.wait_ge(xr_ready, 1)
            move_x(sp, range(BY_SP[0]))
            load_x(1, P)
            sp.wait_ge(xr_ready, 2)
            sp.wait_ge(xp_lo_ready, 1)
            move_x(sp, range(BY_SP[1]))
            sp.wait_ge(turned, 2)
            move_h(sp)
            load_x(2, 2 * P)
            sp.wait_ge(xr_ready, 3)
            sp.wait_ge(xp_lo_ready, 2)
            move_x(sp)
            load_x(3, 3 * P)
            sp.wait_ge(turned, 4)
            sp.wait_ge(h_ready, 1)
            move_h(sp)

            def slot(t, m):
                if not isinstance(t, int) or t > 0:
                    sp.wait_ge(y_ready, t)
                    store((m + 1) % 2, (t - 1) * P)
                first = isinstance(t, int) and t == 0
                if not isinstance(t, int) or t + AHEAD < TILES:
                    if first:
                        sp.wait_ge(xp_lo_ready, 3)
                    else:
                        load_x((m + AHEAD) % UNROLL, (t + AHEAD) * P)
                    sp.wait_ge(xr_ready, t + AHEAD + 1)
                    move_x(sp)
                if not isinstance(t, int) or t + 2 < TILES:
                    sp.wait_ge(turned, 2 * t + 6)
                    move_h(sp)

            slot(0, 0)
            with sp.Fori(0, (TAIL - 1) // UNROLL) as i:
                for k in range(UNROLL):
                    slot(i * UNROLL + (k + 1), (k + 1) % UNROLL)
            for t in range(TAIL, TILES):
                slot(t, t % UNROLL)
            for i in range(NB):
                a, z = max(BOUNDS[i], HEAD) - HEAD, BOUNDS[i + 1] - HEAD
                sp.wait_ge(y_part_ready, i + 1)
                sp.dma_start(out_rows[(TILES - 1) * P:TILES * P, a:z], y_sb[:, 1, a:z]).then_inc(y_free[1], 16)
            sp.wait_ge(y_free[0], 16 + 16 * TILES // 2)
            sp.wait_ge(y_free[1], 16 + 16 * (TILES // 2 - 1 + NB))

        @block.gpsimd
        def _(pool):
            nc.gpsimd.memset(ident[:], 0.0).then_inc(pool_step, 1)
            pool.wait_ge(pool_step, 1)
            nc.gpsimd.affine_select(out=ident[:], in_=ident[:], compare_op=ALU.not_equal, fill=1.0,
                                    base=0, pattern=[[-1, P]], channel_multiplier=1).then_inc(ident_ready, 1)

            pool.dma_start(cond_nat[:], cond).then_inc(cond_loaded, 16)
            pool.dma_start(cw_nat[:], c_weight).then_inc(cond_loaded, 16)
            pool.dma_start(bias_sb[:], bias.rearrange("(a o) -> a o", a=1).broadcast_to([N, C_OUT])
                           ).then_inc(cond_loaded, 16)
            pool.dma_start(head_nat[0:EXPERTS, :], Wr).then_inc(head_loaded, 16)
            pool.dma_start(head_nat[EXPERTS:HEAD, :], A.rearrange("e r l -> (e r) l")).then_inc(head_loaded, 16)
            pool.wait_ge(edges_ready, 3)
            pool.wait_ge(xr_ready, 1)
            move_x(pool, range(BY_SP[0], GN), sp_moves=False)
            x_moved(pool, 0)
            for mt in range(W_BUFS - 1, MT):
                if mt == MT - 2:
                    pool.wait_ge(hq_loaded, 16 * JB)
                if mt >= W_BUFS:
                    pool.wait_ge(setup_done, place("w", (mt - W_BUFS, 1)) + 1)
                load_w(pool, mt)
                if mt == MT - 3:
                    pool.wait_ge(xr_ready, 2)
                    pool.wait_ge(xp_lo_ready, 1)
                    move_x(pool, range(BY_SP[1], GN), sp_moves=False)
            for e in range(EXPERTS):
                pool.dma_start(bm_nat[:, :, e, :], Bm[e].rearrange("(m p) r -> p m r", p=P)).then_inc(up_loaded, 16)
            pool.dma_start(b_nat[:], b.rearrange("(m p) -> p m", p=P), allow_slow_non_contiguous=True
                           ).then_inc(up_loaded, 16)

        @block.tensor
        def _(pe):
            def turn(out_ap, in_ap):
                n = in_ap.shape[0]
                return pe.transpose(out_ap, in_ap, ident[0:n, 0:n])

            def convolve(b, n, unused):
                pe.wait_ge(xp_lo_ready, n)
                unused()
                out_b = ps[:, PREP + b, :].rearrange("p (s g j) -> p g s j", s=PAIR, g=GB)
                for gg in range(GB):
                    g = b * GB + gg
                    for i in range(2):
                        for lhs, rhs in ((toep_hi, xp_hi), (toep_lo, xp_hi), (toep_hi, xp_lo)):
                            last = pe.matmul(out_b[:, gg], lhs[:, i, g, :, :].rearrange("p r o -> p (r o)"),
                                             rhs[:, :, g, i:i + P],
                                             start=(i == 0 and lhs is toep_hi and rhs is xp_hi),
                                             stop=(i == 1 and rhs is xp_lo))
                last.then_inc(conv_done, 1)

            def product(buf, i, rs):
                a, z = BOUNDS[i], BOUNDS[i + 1]
                acc = ps[:, NB * buf + i, 0:z - a]
                for r in rs:
                    for lhs, rhs in ((h_hi, w_hi), (h_hi, w_lo), (h_lo, w_hi)):
                        last = pe.matmul(acc, lhs[:, buf, r, :], rhs[:, r, a:z],
                                         start=(r == 0 and lhs is h_hi and rhs is w_hi),
                                         stop=(r == R - 1 and lhs is h_lo))
                if rs[-1] == R - 1 and i == 0:
                    last.then_inc(head_done, 1)

            def lora_up(buf, banks):
                for i in banks:
                    a = max(BOUNDS[i], HEAD)
                    z = BOUNDS[i + 1]
                    pe.matmul(ps[:, NB * buf + i, a - BOUNDS[i]:z - BOUNDS[i]], mix_t[:], up[:, a - HEAD:z - HEAD],
                              start=False, stop=True, skip_group_check=True).then_inc(y_done, 1)

            def setup(k):
                kind, index = SETUP[k]
                bank = setup_bank(k)
                before = [n for n in range(k) if BANKS[n] == BANKS[k]]
                if before:
                    taken(pe, before[-1])
                if kind == "toep":
                    pe.wait_ge(band_ready, 2 * R)
                    for r in range(R):
                        last = turn(bank[:, r * C_OUT:(r + 1) * C_OUT],
                                    band[:, r, index, :, :].rearrange("p c l -> p (c l)"))
                elif kind == "cond":
                    pe.wait_ge(cond_loaded, 48)
                    turn(bank[:, 0:N], cond_nat[:])
                    last = turn(bank[:, N:N + C_OUT], cw_nat[:])
                elif kind == "ctx":
                    taken(pe, place("cond", 0))
                    last = pe.matmul(bank[0:N, 0:C_OUT], cond_t[:, 0:N], cond_t[:, N:N + C_OUT],
                                     start=True, stop=True)
                elif kind == "shift":
                    if index == 0:
                        pe.wait_ge(edges_ready, 4)
                    pe.wait_ge(diag_ready, 2 * index + 2)
                    for diag in (diag_hi, diag_lo):
                        last = pe.matmul(bank, ones[:], diag[:].rearrange("p n o -> p (n o)"),
                                         start=(diag is diag_hi), stop=(diag is diag_lo))
                elif kind == "head":
                    pe.wait_ge(head_loaded, 32)
                    src = head_nat[:].rearrange("p (j r) -> p r j", r=R)
                    for r in range(R):
                        last = turn(bank[:, r * HEAD:(r + 1) * HEAD], src[:, r, :])
                elif kind == "w":
                    mt, half = index
                    if half == 0:
                        pe.wait_ge(w_loaded[mt], 16)
                    src = w_nat[:, mt % W_BUFS, :].rearrange("p (j r) -> p r j", r=R)
                    for i in range(RB):
                        last = turn(bank[:, i * P:(i + 1) * P], src[:, half * RB + i, :])
                elif kind == "up":
                    if index == 0:
                        pe.wait_ge(up_parts, 5)
                    for i in range(MT // 2):
                        last = turn(bank[:, i * P:(i + 1) * P], up_nat[:, index * MT // 2 + i, :])
                last.then_inc(setup_done, 1)

            def keep_busy(count, lhs, rhs):
                for _ in range(count):
                    pe.matmul(ps[:, PREP + 1, 0:rhs.shape[1]], lhs, rhs, start=True, stop=True)

            pe.wait_ge(edges_ready, 4)
            keep_busy(22, ones[:], ones[:])

            pe.wait_ge(ident_ready, 1)
            for group in BEFORE_0:
                setup(place(*group))
            taken(pe, place("toep", 1))
            convolve(0, 1, lambda: None)
            convolve(1, 1, lambda: None)
            for group in BEFORE_1:
                setup(place(*group))
            pe.wait_ge(turned, 2)
            keep_busy(20, toep_hi[:, 0, 0, :, :].rearrange("p r o -> p (r o)"),
                      toep_hi[:, 0, :, :, :].rearrange("p g r o -> p (g r o)"))
            convolve(0, 2, lambda: None)
            convolve(1, 2, lambda: None)

            def tile(t, m):
                buf = m % 2
                first = isinstance(t, int) and t == 0
                ahead = not isinstance(t, int) or t + 2 < TILES
                at_setup = [(0, 2), (0, 4), (0, 6), (1, 0), (1, 1), (1, 4), (1, 5), (1, 7), (2, 3)]
                at_conv_0, at_conv_1, at_mix = ((1, 6), (2, 1), (2, 6)) if first else ((1, 2), (1, 5), (2, 3))
                at_up = (2, 7) if first else (2, 6)
                if isinstance(t, int) and t == TILES - 1:
                    at_mix, at_up = (2, 0), (2, 2)

                def bank_0_unused():
                    pe.wait_ge(turned, 2 * t + 3)
                    if not first:
                        pe.wait_ge(mix_t_ready, t)

                for i in range(NB):
                    if first:
                        taken(pe, place("w", (W_NEED[i + 1] - 1, 1)))
                    if first and i == 0:
                        taken(pe, place("shift", 0))
                        taken(pe, n_wide - 1)
                    if i == 0:
                        pe.wait_ge(h_lo_ready, t + 1)
                    for r in range(R):
                        product(buf, i, (r,))
                        if first and (i, r) in at_setup:
                            setup(place(*IN_P[at_setup.index((i, r))]))
                        if (i, r) == at_conv_0 and ahead:
                            convolve(0, t + 3, bank_0_unused)
                        if (i, r) == at_conv_1 and ahead:
                            convolve(1, t + 3, lambda: pe.wait_ge(turned, 2 * t + 4))
                        if (i, r) == at_mix:
                            if ahead:
                                pe.wait_ge(turned, 2 * t + 5)
                            pe.wait_ge(mix_ready, t + 1)
                            turn(ps[:, PREP, 0:P], mix_parts[:]).then_inc(mix_turned, 1)
                        if (i, r) == at_up:
                            if first:
                                taken(pe, place("up", 1))
                            pe.wait_ge(mix_t_ready, t + 1)
                            lora_up(buf, range(NB - 1))
                lora_up(buf, (NB - 1,))

            tile(0, 0)
            with pe.Fori(0, (TAIL - 1) // UNROLL) as i:
                for k in range(UNROLL):
                    tile(i * UNROLL + (k + 1), (k + 1) % UNROLL)
            for t in range(TAIL, TILES):
                tile(t, t % UNROLL)

        @block.scalar
        def _(act):
            for mt in range(W_BUFS - 1):
                load_w(act, mt)
            act.wait_ge(edges_ready, 1)
            nc.scalar.copy(gate[:, 0:1], gate[:, 1:2])

            def reorder_x(t, m):
                act.wait_ge(x_loaded[m], loads(t, m))
                src = x_sb[:, m, :].rearrange("p (b r) -> p r b", r=R)
                nc.scalar.copy(xr[:, 0:HALF, 1:P + 1], src[:, HALF:R, :])
                nc.scalar.copy(xr[:, HALF:R, 0:P], src[:, 0:HALF, :]).then_inc(xr_ready, 1)

            def split_x(t):
                x_moved(act, t)
                if not isinstance(t, int) or t > 0:
                    act.wait_ge(conv_done, 2 * t)
                nc.scalar.copy(xp_hi[:], xp[:]).then_inc(xp_hi_ready, 1)

            def round_h(buf, t):
                act.wait_ge(h_ready, t + 1)
                nc.scalar.copy(h_hi[:, buf, :, :], h32[:]).then_inc(h_hi_ready, 1)

            def setup(k):
                kind, index = SETUP[k]
                bank = setup_bank(k)
                act.wait_ge(setup_done, k + 1)
                if kind == "toep":
                    nc.scalar.copy(toep_hi[:, index, :, :, :].rearrange("p g r o -> p r g o"),
                                   bank.rearrange("p (r g o) -> p r g o", r=R, g=G)).then_inc(w_hi_ready, 1)
                elif kind == "cond":
                    nc.scalar.copy(cond_t[:], bank[:, 0:N + C_OUT]).then_inc(act_took, 1)
                elif kind == "shift":
                    nc.scalar.copy(shift_all[:, index * BANK:(index + 1) * BANK], bank).then_inc(act_took, 1)
                elif kind == "head":
                    nc.scalar.copy(w_hi[:, :, 0:HEAD],
                                   bank[:, 0:R * HEAD].rearrange("p (r c) -> p r c", r=R)).then_inc(w_hi_ready, 1)
                elif kind == "w":
                    mt, half = index
                    a = HEAD + mt * P
                    nc.scalar.copy(w_hi[:, half * RB:(half + 1) * RB, a:a + P],
                                   bank.rearrange("p (r c) -> p r c", r=RB)).then_inc(w_hi_ready, 1)
                elif kind == "up":
                    nc.scalar.copy(up[:, index * BANK:(index + 1) * BANK], bank).then_inc(act_took, 1)

            def groups(names):
                for group in names:
                    if group[0] != "ctx":
                        setup(place(*group))

            reorder_x(0, 0)
            groups(BEFORE_0[:-4])
            split_x(0)
            groups(BEFORE_0[-4:])
            reorder_x(1, 1)
            groups(BEFORE_1)
            split_x(1)
            round_h(0, 0)
            reorder_x(2, 2)
            groups(IN_P[:5])
            split_x(2)
            groups(IN_P[5:-2])
            reorder_x(3, 3)
            groups(IN_P[-2:-1])

            def tile(t, m):
                buf = m % 2
                if not isinstance(t, int) or 0 < t < TILES - 2:
                    split_x(t + 2)
                if not isinstance(t, int) or t + 1 < TILES:
                    round_h(1 - buf, t + 1)
                if not isinstance(t, int) or 0 < t < TAIL:
                    reorder_x(t + AHEAD, (m + AHEAD) % UNROLL)
                act.wait_ge(max_ready, t + 1)
                nc.scalar.activation(gate[:, 4:4 + EXPERTS], ps[:, NB * buf, 0:EXPERTS], ACT.Exp,
                                     bias=gate[:, 0:1], accum_out=gate[:, 1:2]).then_inc(exp_ready, 1)
                if isinstance(t, int) and t == 0:
                    groups(IN_P[-1:])
                act.wait_ge(mix_turned, t + 1)
                nc.scalar.copy(mix_t[:], ps[:, PREP, 0:P]).then_inc(mix_t_ready, 1)

            tile(0, 0)
            with act.Fori(0, (TAIL - 1) // UNROLL) as i:
                for k in range(UNROLL):
                    tile(i * UNROLL + (k + 1), (k + 1) % UNROLL)
            for t in range(TAIL, TILES):
                tile(t, t % UNROLL)

        @block.vector
        def _(dve):
            def split_x(t):
                dve.wait_ge(xp_hi_ready, t + 1)
                nc.vector.tensor_tensor(xp_lo[:], xp[:], xp_hi[:].bitcast(F32), ALU.subtract).then_inc(xp_lo_ready, 1)

            def turn_conv(b, t):
                dve.wait_ge(conv_done, 2 * t + b + 1)
                nc.vector.transpose(ht[:, :, b, :, :].rearrange("p j c i -> p c j i"),
                                    ps[:, PREP + b, :].rearrange("p (c i j) -> p c j i", j=JB, i=Q)
                                    ).then_inc(turned, 1)

            def add_shift(t):
                if not isinstance(t, int) or t > 0:
                    dve.wait_ge(h_lo_ready, t)
                dve.wait_ge(hq_loaded, 16 * JB * (t + 1))
                width = PAIR * C_OUT
                add = shift_all[:, t * width:(t + 1) * width] if isinstance(t, int) else \
                    shift_all[:, bass.ds(t * width, width)]
                add = add.rearrange("p (q s b g o) -> p q b s g o", q=1, s=PAIR, b=2, g=GB)
                src = hq[:].rearrange("p q (b s g r o) -> p q b s g r o", b=2, s=PAIR, g=GB, r=R2)
                dst = h32[:].rearrange("p (q r) (s b g o) -> p q r b s g o", r=R2, s=PAIR, b=2, g=GB)
                for b in range(2):
                    for r in range(R2):
                        last = nc.vector.tensor_tensor(dst[:, :, r, b], src[:, :, b, :, :, r, :],
                                                       add[:, :, b].broadcast_to([P, JB, PAIR, GB, O]), ALU.add)
                last.then_inc(h_ready, 1)

            def split_h(buf, t):
                dve.wait_ge(h_hi_ready, t + 1)
                nc.vector.tensor_tensor(h_lo[:, buf, :, :], h32[:], h_hi[:, buf, :, :].bitcast(F32),
                                        ALU.subtract).then_inc(h_lo_ready, 1)

            def setup(k):
                kind, index = SETUP[k]
                bank = setup_bank(k)
                if kind == "ctx":
                    dve.wait_ge(setup_done, k + 1)
                    nc.vector.tensor_tensor(shift[:], bank[0:N, 0:C_OUT], bias_sb[:], ALU.add).then_inc(dve_took, 1)
                    taken(dve, k)
                    nc.vector.tensor_copy(shift_hi[:], shift[:]).then_inc(shift_step, 1)
                    dve.wait_ge(shift_step, 1)
                    nc.vector.tensor_tensor(shift_lo[:], shift[:], shift_hi[:].bitcast(F32),
                                            ALU.subtract).then_inc(shift_step, 1)
                elif kind == "toep":
                    dve.wait_ge(w_hi_ready, hi_count(k))
                    nc.vector.tensor_tensor(toep_lo[:, index, :, :, :].rearrange("p g r o -> p r g o"),
                                            bank.rearrange("p (r g o) -> p r g o", r=R, g=G),
                                            toep_hi[:, index, :, :, :].bitcast(F32).rearrange("p g r o -> p r g o"),
                                            ALU.subtract).then_inc(dve_took, 1)
                elif kind == "head":
                    dve.wait_ge(w_hi_ready, hi_count(k))
                    nc.vector.tensor_tensor(w_lo[:, :, 0:HEAD], bank[:, 0:R * HEAD].rearrange("p (r c) -> p r c", r=R),
                                            w_hi[:, :, 0:HEAD].bitcast(F32), ALU.subtract).then_inc(dve_took, 1)
                elif kind == "w":
                    mt, half = index
                    a = HEAD + mt * P
                    dve.wait_ge(w_hi_ready, hi_count(k))
                    rs = slice(half * RB, (half + 1) * RB)
                    nc.vector.tensor_tensor(w_lo[:, rs, a:a + P], bank.rearrange("p (r c) -> p r c", r=RB),
                                            w_hi[:, rs, a:a + P].bitcast(F32), ALU.subtract).then_inc(dve_took, 1)

            def diagonal(index):
                a = index * DIAG
                if index == 0:
                    dve.wait_ge(ident_ready, 1)
                    dve.wait_ge(shift_step, 2)
                else:
                    dve.wait_ge(setup_done, place("shift", index - 1) + 1)
                for part, diag in ((shift_hi, diag_hi), (shift_lo, diag_lo)):
                    nc.vector.tensor_tensor(
                        diag[:],
                        part[:].bitcast(F32).rearrange("p (n o) -> p n o", n=1).broadcast_to([N, DIAG, C_OUT]),
                        ident[0:N, a:a + DIAG].rearrange("p (n o) -> p n o", o=1).broadcast_to([N, DIAG, C_OUT]),
                        ALU.mult).then_inc(diag_ready, 1)

            def up_columns():
                bm = bm_nat[:].rearrange("p m e r -> p m (e r)")
                bb = b_nat[:].rearrange("p (m a) -> p m a", a=1)
                dve.wait_ge(up_loaded, 16 * (EXPERTS + 1))
                dve.wait_ge(fill_step, 4)
                nc.vector.tensor_copy(up_nat[:, :, G_HI:G_HI + ER].bitcast(F32R), bm).then_inc(up_parts, 1)
                nc.vector.tensor_copy(up_nat[:, :, G_LO:G_LO + ER].bitcast(F32R), bm).then_inc(up_parts, 1)
                nc.vector.tensor_copy(up_nat[:, :, ONES:ONES + 1].bitcast(F32R), bb).then_inc(up_parts, 1)
                dve.wait_ge(up_parts, 3)
                nc.vector.tensor_tensor(up_nat[:, :, G_HI2:G_HI2 + ER], bm, up_nat[:, :, G_HI:G_HI + ER],
                                        ALU.subtract).then_inc(up_parts, 1)
                nc.vector.tensor_tensor(up_nat[:, :, ONES + 1:ONES + 2], bb, up_nat[:, :, ONES:ONES + 1],
                                        ALU.subtract).then_inc(up_parts, 1)

            nc.vector.memset(gate[:], 0.0).then_inc(edges_ready, 1)
            nc.vector.memset(xr[:, 0:HALF, 0:1], 0.0).then_inc(edges_ready, 1)
            nc.vector.memset(xr[:, HALF:R, P:P + 1], 0.0).then_inc(edges_ready, 1)
            nc.vector.memset(ones[:].bitcast(F32), 1.0).then_inc(edges_ready, 1)
            nc.vector.memset(mix_parts[:, ONES:P], 0.0).then_inc(fill_step, 1)
            nc.vector.memset(band[:], 0.0).then_inc(fill_step, 1)
            dve.wait_ge(fill_step, 2)
            nc.vector.memset(mix_parts[:, ONES:ONES + 2], 1.0).then_inc(fill_step, 1)
            taps = conv_nat[:].rearrange("p (c k) -> p c k", k=K)
            dve.wait_ge(conv_loaded, 16)
            for r in range(R):
                nc.vector.tensor_copy(band[:, r, 0, :, r:R], taps[:, :, 0:R - r]).then_inc(band_ready, 1)
                nc.vector.tensor_copy(band[:, r, 1, :, 0:r + 1], taps[:, :, R - r:K]).then_inc(band_ready, 1)
            nc.vector.memset(up_nat[:, :, ONES:P], 0.0).then_inc(fill_step, 1)
            nc.vector.memset(gates[:], 0.0).then_inc(y_free[0], 16)
            nc.vector.memset(mixed[:], 0.0).then_inc(y_free[1], 16)

            def groups(names):
                for group in names:
                    if group[0] not in BY_ACT:
                        setup(place(*group))

            groups(BEFORE_0[:-4])
            split_x(0)
            groups(BEFORE_0[-4:])
            turn_conv(0, 0)
            turn_conv(1, 0)
            diagonal(0)
            groups(BEFORE_1)
            taken(dve, place("shift", 0))
            add_shift(0)
            split_x(1)
            split_h(0, 0)
            turn_conv(0, 1)
            turn_conv(1, 1)
            diagonal(1)
            groups(IN_P[:4])
            up_columns()
            split_x(2)
            diagonal(2)

            def gating(buf, t):
                logits = ps[:, NB * buf, 0:EXPERTS]
                down = ps[:, NB * buf, EXPERTS:HEAD].rearrange("p (e r) -> p e r", e=EXPERTS)
                base = t * GATE_STEPS
                dve.wait_ge(head_done, t + 1)
                nc.vector.tensor_reduce(gate[:, 0:1], logits, AX_X, ALU.max, negate=True).then_inc(max_ready, 1)
                dve.wait_ge(exp_ready, t + 1)
                nc.vector.reciprocal(gate[:, 2:3], gate[:, 1:2]).then_inc(gate_step, 1)
                dve.wait_ge(gate_step, base + 1)
                nc.vector.tensor_scalar(gates[:], gate[:, 4:4 + EXPERTS], gate[:, 2:3], LORA_SCALE,
                                        ALU.mult, ALU.mult).then_inc(gate_step, 1)
                dve.wait_ge(gate_step, base + 2)
                nc.vector.tensor_tensor(mixed[:].rearrange("p (e r) -> p e r", e=EXPERTS), down,
                                        gates[:].rearrange("p (e r) -> p e r", r=1)
                                        .broadcast_to([P, EXPERTS, RANK]), ALU.mult).then_inc(gate_step, 1)
                dve.wait_ge(gate_step, base + 3)
                nc.vector.tensor_copy(mix_parts[:, G_HI:G_HI + ER].bitcast(F32R), mixed[:]).then_inc(gate_step, 1)
                nc.vector.tensor_copy(mix_parts[:, G_HI2:G_HI2 + ER].bitcast(F32R), mixed[:]).then_inc(gate_step, 1)
                dve.wait_ge(gate_step, base + 5)
                nc.vector.tensor_tensor(mix_parts[:, G_LO:G_LO + ER], mixed[:], mix_parts[:, G_HI:G_HI + ER],
                                        ALU.subtract).then_inc(mix_ready, 1)

            def finish(t, m, parts=False):
                buf = m % 2
                dve.wait_ge(y_free[buf], frees(t, buf))
                for i in range(NB):
                    a, z = max(BOUNDS[i], HEAD), BOUNDS[i + 1]
                    dve.wait_ge(y_done, NB * t + i + 1)
                    last = nc.vector.tensor_tensor(y_sb[:, buf, a - HEAD:z - HEAD],
                                                   ps[:, NB * buf + i, a - BOUNDS[i]:z - BOUNDS[i]],
                                                   x_sb[:, m, a - HEAD:z - HEAD], ALU.add)
                    if parts:
                        last.then_inc(y_part_ready, 1)
                if not parts:
                    last.then_inc(y_ready, 1)

            def tile(t, m):
                buf = m % 2
                first = isinstance(t, int) and t == 0
                if not first:
                    finish(t - 1, (m - 1) % UNROLL)
                if not isinstance(t, int) or 0 < t < TILES - 2:
                    split_x(t + 2)
                if not isinstance(t, int) or t + 1 < TILES:
                    add_shift(t + 1)
                if not isinstance(t, int) or t + 2 < TILES:
                    turn_conv(0, t + 2)
                if first:
                    diagonal(3)
                if not isinstance(t, int) or t + 1 < TILES:
                    split_h(1 - buf, t + 1)
                gating(buf, t)
                if not isinstance(t, int) or t + 2 < TILES:
                    turn_conv(1, t + 2)

            tile(0, 0)
            with dve.Fori(0, (TAIL - 1) // UNROLL) as i:
                for k in range(UNROLL):
                    tile(i * UNROLL + (k + 1), (k + 1) % UNROLL)
            for t in range(TAIL, TILES):
                tile(t, t % UNROLL)
            finish(TILES - 1, (TILES - 1) % UNROLL, parts=True)


_INS = ['x', 'cond_128', 'fside_S_0', 'L0_cond_weight', 'L0_cond_c_weight', 'L0_ffn_W', 'L0_ffn_b',
        'L0_ffn_A', 'L0_ffn_Bm', 'L0_ffn_Wr']
_OUTS = [((32, 64, 1024), 'float32')]


def kernel(**inputs):
    import numpy as _np
    import concourse.bacc as _bacc
    from concourse import mybir as _mybir
    from concourse.bass_utils import run_bass_kernel_spmd as _run

    nc = _bacc.Bacc("TRN2", target_bir_lowering=False, num_devices=1)
    arrays, args = {}, []
    for name in _INS:
        a = _np.ascontiguousarray(inputs[name])
        arrays[f"in_{name}_dram"] = a
        args.append(nc.dram_tensor(f"in_{name}_dram", a.shape, _mybir.dt.from_np(a.dtype), kind="ExternalInput").ap())
    for i, (shape, dtype) in enumerate(_OUTS):
        dt = _mybir.dt.from_np(_np.dtype(dtype))
        args.append(nc.dram_tensor(f"out_{i}_dram", shape, dt, kind="ExternalOutput").ap())
    adaln_ffn(nc, *args)
    r = _run(nc, [arrays], core_ids=[0])
    got = tuple(r.results[0][f"out_{i}_dram"] for i in range(len(_OUTS)))
    return got[0]
```
